# Optimizing a Trainium2 kernel written in Bass

```python
import numpy as np
import jax
import jax.numpy as jnp

def _softmax(x, axis=-1):
    return jax.nn.softmax(x, axis=axis)

def _gelu(x):
    return jax.nn.gelu(x, approximate=True)

def _silu(x):
    return jax.nn.silu(x)

def _sigmoid(x):
    return jax.nn.sigmoid(x)

def _layernorm(x, axis=-1, eps=1e-05):
    m = jnp.mean(x, axis=axis, keepdims=True)
    v = jnp.var(x, axis=axis, keepdims=True)
    return (x - m) / jnp.sqrt(v + eps)

def _scatter_add(tgt, idx, src, axis=0):
    return tgt.at[idx].add(src)

def _segment_sum(src, seg, n):
    return jax.ops.segment_sum(src, seg, n)
kernel_name = 'mk_prb_d1_jaxref_r8_260678'

def setup_inputs(seed: int=0):
    np.random.seed(seed)
    _w = jnp.asarray

    def _L0_attn_setup():
        import jax, jax.numpy as jnp
        import numpy as np
        DIM = 128
        HEADS = 16
        DIM_HEAD = 64
        SOFTCLAMP = 50.0

        def _rmsnorm(x, w):
            eps = jnp.finfo(x.dtype).eps
            var = jnp.mean(jnp.square(x), axis=-1, keepdims=True)
            return x * jax.lax.rsqrt(var + eps) * w

        def _head_rmsnorm(x, gamma):
            norm = jnp.linalg.norm(x, axis=-1, keepdims=True)
            normed = x / jnp.maximum(norm, 1e-12)
            scale = (gamma + 1.0) * DIM_HEAD ** 0.5
            return normed * scale[None, :, None, :]
        key = jax.random.key(seed)
        ks = jax.random.split(key, 7)
        b, n = (4, 256)
        di = HEADS * DIM_HEAD
        s = 0.02
        return {'tokens': jax.random.normal(ks[0], (b, n, DIM), dtype=jnp.float32), 'norm_w': jnp.ones((DIM,), dtype=jnp.float32), 'Wq': jax.random.normal(ks[1], (DIM, di), dtype=jnp.float32) * s, 'Wkv': jax.random.normal(ks[2], (DIM, 2 * di), dtype=jnp.float32) * s, 'Wo': jax.random.normal(ks[3], (di, DIM), dtype=jnp.float32) * s, 'q_gamma': jnp.zeros((HEADS, DIM_HEAD), dtype=jnp.float32), 'k_gamma': jnp.zeros((HEADS, DIM_HEAD), dtype=jnp.float32)}
    _L0_attn_in = _L0_attn_setup()

    def _L0_ffn_setup():
        import jax, jax.numpy as jnp
        import numpy as np
        LORA_DIM = 16
        LORA_TOKEN_INDEX = 1
        B, S, D, H = (4, 256, 128, 512)
        key = jax.random.key(seed)
        ks = jax.random.split(key, 6)
        x = jax.random.normal(ks[0], (B, S, D), dtype=jnp.float32)
        W1 = jax.random.normal(ks[1], (H, D), dtype=jnp.float32) * 0.02
        b1 = jnp.zeros((H,), dtype=jnp.float32)
        W2 = jax.random.normal(ks[2], (D, H), dtype=jnp.float32) * 0.02
        b2 = jnp.zeros((D,), dtype=jnp.float32)
        scale = jnp.asarray(0.001, dtype=jnp.float32)
        return {'x': x, 'W1': W1, 'b1': b1, 'W2': W2, 'b2': b2, 'scale': scale}
    _L0_ffn_in = _L0_ffn_setup()
    _d = {'L0_attn_tokens': _L0_attn_in['tokens'], 'L0_attn_norm_w': _L0_attn_in['norm_w'], 'L0_attn_Wq': _L0_attn_in['Wq'], 'L0_attn_Wkv': _L0_attn_in['Wkv'], 'L0_attn_Wo': _L0_attn_in['Wo'], 'L0_attn_q_gamma': _L0_attn_in['q_gamma'], 'L0_attn_k_gamma': _L0_attn_in['k_gamma'], 'L0_ffn_W1': _L0_ffn_in['W1'], 'L0_ffn_b1': _L0_ffn_in['b1'], 'L0_ffn_W2': _L0_ffn_in['W2'], 'L0_ffn_b2': _L0_ffn_in['b2'], 'L0_ffn_scale': _L0_ffn_in['scale']}
    _x0 = _d['L0_attn_tokens']
    _d['L0_attn_tokens'] = jax.random.normal(jax.random.fold_in(jax.random.key(seed), 1), (32, 256, 128), dtype=_x0.dtype)
    del _x0
    return _d

def reference(L0_attn_tokens, L0_attn_norm_w, L0_attn_Wq, L0_attn_Wkv, L0_attn_Wo, L0_attn_q_gamma, L0_attn_k_gamma, L0_ffn_W1, L0_ffn_b1, L0_ffn_W2, L0_ffn_b2, L0_ffn_scale):

    def _L0_attn_ref(tokens, norm_w, Wq, Wkv, Wo, q_gamma, k_gamma):
        import jax, jax.numpy as jnp
        import numpy as np
        DIM = 128
        HEADS = 16
        DIM_HEAD = 64
        SOFTCLAMP = 50.0

        def _rmsnorm(x, w):
            eps = jnp.finfo(x.dtype).eps
            var = jnp.mean(jnp.square(x), axis=-1, keepdims=True)
            return x * jax.lax.rsqrt(var + eps) * w

        def _head_rmsnorm(x, gamma):
            norm = jnp.linalg.norm(x, axis=-1, keepdims=True)
            normed = x / jnp.maximum(norm, 1e-12)
            scale = (gamma + 1.0) * DIM_HEAD ** 0.5
            return normed * scale[None, :, None, :]
        b, n, _ = tokens.shape
        x = _rmsnorm(tokens, norm_w)
        q = x @ Wq
        kv = x @ Wkv
        k, v = jnp.split(kv, 2, axis=-1)
        split = lambda t: t.reshape(b, n, HEADS, DIM_HEAD).transpose(0, 2, 1, 3)
        q, k, v = (split(q), split(k), split(v))
        q = _head_rmsnorm(q, q_gamma)
        k = _head_rmsnorm(k, k_gamma)
        sim = jnp.einsum('bhid,bhjd->bhij', q, k)
        sim = jnp.tanh(sim / SOFTCLAMP) * SOFTCLAMP
        sim = sim * DIM_HEAD ** (-0.5)
        attn = jax.nn.softmax(sim, axis=-1)
        out = jnp.einsum('bhij,bhjd->bhid', attn, v)
        out = out.transpose(0, 2, 1, 3).reshape(b, n, HEADS * DIM_HEAD)
        return out @ Wo

    def _L0_ffn_ref(x, W1, b1, W2, b2, scale):
        import jax, jax.numpy as jnp
        import numpy as np
        LORA_DIM = 16
        LORA_TOKEN_INDEX = 1
        B, S, D, H = (4, 256, 128, 512)
        Bx, Sx, Dx = x.shape
        Hx = W1.shape[0]
        lt = jax.lax.dynamic_slice_in_dim(x, LORA_TOKEN_INDEX, LORA_DIM, axis=1)
        even = lt[:, ::2, :]
        odd = lt[:, 1::2, :]
        m1 = (even[:, :4, :, None] * odd[:, :4, None, :]).reshape(Bx, Hx, Dx)
        m2 = (even[:, 4:, :, None] * odd[:, 4:, None, :]).reshape(Bx, Dx, Hx)
        h = jnp.einsum('bsd,hd->bsh', x, W1) + scale * jnp.einsum('bsd,bhd->bsh', x, m1) + b1
        h = jax.nn.gelu(h, approximate=False)
        out = jnp.einsum('bsh,oh->bso', h, W2) + scale * jnp.einsum('bsh,boh->bso', h, m2) + b2
        return out
    x = L0_attn_tokens
    xn = _layernorm(x, axis=-1)
    x = x + _L0_attn_ref(xn, L0_attn_norm_w, L0_attn_Wq, L0_attn_Wkv, L0_attn_Wo, L0_attn_q_gamma, L0_attn_k_gamma) + _L0_ffn_ref(xn, L0_ffn_W1, L0_ffn_b1, L0_ffn_W2, L0_ffn_b2, L0_ffn_scale)
    return x

_drawn_inputs = setup_inputs


def setup_inputs(seed=0):
    import zlib

    import numpy as np

    out = dict(_drawn_inputs(seed))
    spreads = {'L0_attn_norm_w': (1.0, 0.6),
     'L0_attn_q_gamma': (0.0, 0.8),
     'L0_attn_k_gamma': (0.0, 0.8),
     'L0_ffn_b1': (0.0, 0.322),
     'L0_ffn_b2': (0.0, 0.1)}
    factors = {'L0_attn_Wq': 3.341, 'L0_attn_Wkv': 2.957, 'L0_attn_Wo': 2.948}
    for name, (base, spread) in spreads.items():
        noise = np.random.default_rng([zlib.crc32(name.encode()), seed]).standard_normal(out[name].shape)
        drawn = base * np.exp(spread * noise) if base else spread * noise
        out[name] = jnp.asarray(drawn.astype(out[name].dtype))
    for name, factor in factors.items():
        out[name] = (out[name] * factor).astype(out[name].dtype)
    return out
```

```python
from contextlib import ExitStack

import concourse.bass as bass
from concourse import mybir

F32 = mybir.dt.float32
F32R = mybir.dt.float32r
BF16 = mybir.dt.bfloat16
F16 = mybir.dt.float16
I32 = mybir.dt.int32
ALU = mybir.AluOpType
ACT = mybir.ActivationFunctionType
AX_X = mybir.AxisListType.X

P = 128
HEADS = 16
DH = 64
PAIRS = HEADS // 2
HIDDEN = 512
HC = HIDDEN // P
RANK = 4
SOFTCLAMP = 50.0
LN_EPS = 1e-5
RMS_EPS = 2.0 ** -23
NORM2_MIN = 1e-24
RSQRT_SEED = float(0x5F3759DF)
LIFT = 4.1588830833596715

AUX = [(0, "xT", 0)]
AUX += [(1 + k // 2, "qk", k) for k in range(8)]
AUX += [(5 + k // 2, "v", k) for k in range(4)]
AUX += [(7 + k // 2, "oT", k) for k in range(4)]
AUX += [(9, "sel", 0), (9, "low", 0), (10, "low", 1), (10, "qkT", 0), (11, "qkT", 1), (11, "qkT", 2),
        (12, "qkT", 3), (12, "qkT", 4), (13, "hid", 0), (13, "hid", 1), (14, "qkT", 5), (14, "qkT", 6), (15, "qkT", 7)]
PER_BATCH = {"xT": 1, "qk": 8, "v": 4, "oT": 4, "sel": 1, "low": 2, "qkT": 8, "hid": 2}
STAGE = {"xT": ("front", 1), "qk": ("front", 1), "v": ("front", 1), "qkT": ("front", 1),
         "oT": ("back", -1), "sel": ("attn", 0), "low": ("attn", 0), "hid": ("attn", 0)}
AUX_BANKS = 2
POOL_HEADS = (2, 5, 8, 11, 14)
SCORE_BANK = [h % 3 for h in range(HEADS - 1)] + [1]
SCORE_BACK = [next(d for d in range(1, HEADS) if SCORE_BANK[h - d] == SCORE_BANK[h]) for h in range(HEADS)]
RING = 4
Y_SLOTS = range(9, 15)


class Step:

    def __init__(self, half, odd, stages):
        self.half, self.odd, self.stages = half, odd, stages

    def batch(self, ahead):
        m = self.odd + ahead
        return 2 * self.half + m, m % 2, self.half + m // 2


def stages_of(n, batches):
    out = set()
    if 0 <= n < batches:
        out.add("attn")
    if 0 <= n + 1 < batches:
        out.add("front")
    if 0 <= n + 2 < batches:
        out.add("norm")
    if 0 <= n + 3 < batches:
        out.add("load")
    if 0 <= n - 1 < batches:
        out.add("back")
    return out


def block_kernel(nc, tokens, norm_w, wq, wkv, wo, q_gamma, k_gamma, w1, b1, w2, b2, scale, out):
    batches, seq, dim = tokens.shape
    TT = seq // P
    assert dim == P and TT == 2 and wq.shape[1] == HEADS * DH and w1.shape[0] == HIDDEN and batches % 2 == 0
    QK = 2 * HEADS * DH
    QKV = QK + HEADS * DH

    with ExitStack() as ctx:
        def sb(name, shape, dt=F32):
            return ctx.enter_context(nc.sbuf_tensor(name, shape, dt))

        def sem(name):
            return ctx.enter_context(nc.semaphore(name))

        ps_scores = ctx.enter_context(nc.psum_tensor("ps_scores", [P, 3, 512], F32))
        ps_o = ctx.enter_context(nc.psum_tensor("ps_o", [P, 2, 512], F32))
        ps_aux = ctx.enter_context(nc.psum_tensor("ps_aux", [P, AUX_BANKS, 512], F32))
        ps_y = ctx.enter_context(nc.psum_tensor("ps_y", [P, 512], F32))

        ident = sb("ident", [P, P])
        w_raw = sb("w_raw", [P, QKV])
        w_hi = sb("w_hi", [P, QKV], F32R)
        w_lo = sb("w_lo", [P, QKV], F32R)
        wo_sb = sb("wo_sb", [P, PAIRS, P])
        w1_raw = sb("w1_raw", [P, HC, P])
        w2_raw = sb("w2_raw", [P, HIDDEN])
        w1T = sb("w1T", [P, HC, P])
        w2T = sb("w2T", [P, HC, P])
        nw_col = sb("nw_col", [P, 1])
        g_raw = sb("g_raw", [PAIRS, 2, P])
        g_row = sb("g_row", [PAIRS, P])
        g_col = sb("g_col", [P, PAIRS])
        b1_raw = sb("b1_raw", [HC, P])
        b1_col = sb("b1_col", [P, HC])
        b2_bc = sb("b2_bc", [P, P])
        scale_col = sb("scale_col", [2 * RANK, 1])
        mask1 = sb("mask1", [2 * RANK, RANK, P])
        mask2 = sb("mask2", [2 * RANK, HC, RANK, P // RANK])
        minus_half = sb("minus_half", [P, 4])
        lift_col = sb("lift_col", [P, 1])
        scratch = sb("scratch", [P, 1])
        newton_c = sb("newton_c", [P, TT * 2 * HEADS])

        x_in = sb("x_in", [P, 2, TT, P])
        x_res = sb("x_res", [P, 2, TT, P])
        x_b2 = sb("x_b2", [P, TT, P])
        stats = sb("stats", [P, TT, 6])
        mean_var = sb("mean_var", [P, TT, 2])
        var_eps = sb("var_eps", [P, 2, TT])
        rstd = sb("rstd", [P, 2, TT])
        xn = sb("xn", [P, 2, TT, P])
        xh = sb("xh", [P, TT, P])
        xnT = sb("xnT", [P, 2, seq])
        xhT_hi = sb("xhT_hi", [P, seq], F32R)
        xhT_lo = sb("xhT_lo", [P, seq], F32R)
        qk = sb("qk", [P, TT, QK])
        sq = sb("sq", [P, 2, 512])
        norm2 = sb("norm2", [P, TT * 2 * HEADS])
        norm2_safe = sb("norm2_safe", [P, TT * 2 * HEADS])
        minus_half_norm2 = sb("minus_half_norm2", [P, TT * 2 * HEADS])
        rnorm = sb("rnorm", [P, TT * 2 * HEADS])
        newton_a = sb("newton_a", [P, TT * 2 * HEADS])
        newton_b = sb("newton_b", [P, TT * 2 * HEADS])
        qT_hi = sb("qT_hi", [P, 2, PAIRS, seq], F16)
        qT_lo = sb("qT_lo", [P, 2, PAIRS, seq], F16)
        kT_hi = sb("kT_hi", [P, 2, PAIRS, seq], F16)
        kT_lo = sb("kT_lo", [P, 2, PAIRS, seq], F16)
        v_hi = sb("v_hi", [P, 2, TT, HEADS, DH + 1], BF16)
        v_lo = sb("v_lo", [P, 2, TT, HEADS, DH], BF16)
        clamped = sb("clamped", [P, RING, TT * seq])
        probs = sb("probs", [P, RING, TT * seq])
        probs_lo = sb("probs_lo", [P, RING, TT * seq], F16)
        rden = sb("rden", [P, 2, 4])
        o_sb = sb("o_sb", [P, 2, TT, HEADS * DH])
        oT = sb("oT", [P, PAIRS, seq])
        sel_rows = sb("sel_rows", [2 * RANK, 2, P])
        low1 = sb("low1", [2 * RANK, RANK, P])
        low2 = sb("low2", [2 * RANK, HC, RANK, P // RANK])
        w1_eff = sb("w1_eff", [P, HC, P])
        w2_eff = sb("w2_eff", [P, 2, HC, P])
        hid = sb("hid", [P, 2, HC, seq])
        y_sb = sb("y_sb", [P, 2, TT, P])

        consts_loaded = sem("consts_loaded")
        ident_made = sem("ident_made")
        masks_made = sem("masks_made")
        setup_made = sem("setup_made")
        setup_turned = sem("setup_turned")
        x_loaded = [sem(f"x_loaded{i}") for i in range(2)]
        res_loaded = [sem(f"res_loaded{i}") for i in range(2)]
        y_stored = [sem(f"y_stored{i}") for i in range(2)]
        stats_made = sem("stats_made")
        meanvar_made = sem("meanvar_made")
        vareps_made = sem("vareps_made")
        rstd_made = sem("rstd_made")
        xn_made = sem("xn_made")
        sq_made = sem("sq_made")
        norm2_made = sem("norm2_made")
        seed_made = sem("seed_made")
        newton_step = sem("newton_step")
        qk_normed = sem("qk_normed")
        scores_done = sem("scores_done")
        clamp_done = sem("clamp_done")
        probs_done = sem("probs_done")
        lo_by_vector = sem("lo_by_vector")
        lo_by_pool = sem("lo_by_pool")
        attended = sem("attended")
        rden_made = sem("rden_made")
        o_normed = sem("o_normed")
        aux_filled = {k: sem(f"{k}_filled") for k in PER_BATCH}
        xT_hi_made = sem("xT_hi_made")
        xT_split = sem("xT_split")
        qk_copied = sem("qk_copied")
        v_hi_made = sem("v_hi_made")
        v_split = sem("v_split")
        qkT_hi_made = sem("qkT_hi_made")
        qkT_split = sem("qkT_split")
        oT_copied = sem("oT_copied")
        sel_copied = sem("sel_copied")
        low_made = sem("low_made")
        weff_made = sem("weff_made")
        gelu_done = sem("gelu_done")
        y_filled = sem("y_filled")
        xb2_made = sem("xb2_made")
        y_added = sem("y_added")

        AUX_READ = {"xT": (xT_split, 1), "qk": (qk_copied, 1), "v": (v_split, 1), "qkT": (qkT_split, 1),
                    "oT": (oT_copied, 1), "sel": (sel_copied, 1), "low": (weff_made, 1), "hid": (gelu_done, 2)}

        def wait(eng, s, value):
            if isinstance(value, int) and value <= 0:
                return
            eng.wait_ge(s, value)

        def wait_bank(eng, st, index):
            for back in range(1, 3 * len(AUX)):
                i = index - back * AUX_BANKS
                rounds, j = i // len(AUX), i % len(AUX)
                if rounds < -1:
                    return
                _, kind, k = AUX[j]
                stage, ahead = STAGE[kind]
                if rounds == 0 and stage in st.stages or rounds < 0 and stage in st.before:
                    s, per = AUX_READ[kind]
                    wait(eng, s, per * PER_BATCH[kind] * st.batch(ahead + rounds)[0] + per * (k + 1))
                    return

        def aux_tasks(st, slot, kinds):
            for i, (s, kind, k) in enumerate(AUX):
                if s == slot and kind in kinds and STAGE[kind][0] in st.stages:
                    yield i, kind, k

        def head_of(st, slot, lag):
            ahead, head = (0, slot - lag) if slot >= lag else (-1, slot - lag + HEADS)
            there = "attn" if ahead == 0 else "back"
            return (ahead, head) if there in st.stages else None

        def plan(run):
            def straight(n):
                st = Step(n // 2, n % 2, stages_of(n, batches))
                st.before = stages_of(n - 1, batches)
                run(st)

            first, last = 3, batches - 4
            for n in range(-2, first):
                straight(n)
            yield first // 2, (last + 1) // 2
            for n in range(last + 1, batches + 1):
                straight(n)

        def run_all(eng, run):
            for start, end in plan(run):
                with eng.Fori(start, end) as i:
                    for odd in (1, 2):
                        st = Step(i, odd, stages_of(3, batches))
                        st.before = st.stages
                        run(st)

        def vector_count(b, h):
            return (HEADS - len(POOL_HEADS)) * b + len([i for i in range(h + 1) if i not in POOL_HEADS])

        block = ctx.enter_context(nc.Block())

        @block.sync
        def _(sp):
            def x_of(b):
                return tokens[bass.ds(b, 1)].rearrange("o (t p) d -> p (o t) d", p=P)

            sp.dma_start(x_in[:, 0], tokens[0].rearrange("(t p) d -> p t d", p=P)).then_inc(x_loaded[0], 16)
            sp.dma_start(x_in[:, 1], tokens[1].rearrange("(t p) d -> p t d", p=P)).then_inc(x_loaded[1], 16)
            sp.dma_start(nw_col[:], norm_w.rearrange("(p o) -> p o", o=1)).then_inc(consts_loaded, 16)
            sp.dma_start(w_raw[:, 0:HEADS * DH], wq).then_inc(consts_loaded, 16)
            sp.dma_start(w_raw[:, HEADS * DH:QKV], wkv).then_inc(consts_loaded, 16)
            sp.dma_start(g_raw[:, 0], q_gamma.rearrange("(p a) d -> p (a d)", a=2)).then_inc(consts_loaded, 16)
            sp.dma_start(g_raw[:, 1], k_gamma.rearrange("(p a) d -> p (a d)", a=2)).then_inc(consts_loaded, 16)
            sp.dma_start(b1_raw[:], b1.rearrange("(c p) -> c p", p=P)).then_inc(consts_loaded, 16)
            sp.dma_start(b2_bc[:], b2.rearrange("(o d) -> o d", o=1).to_broadcast([P, P])).then_inc(consts_loaded, 16)
            sp.dma_start(scale_col[:], scale.rearrange("(o d) -> o d", o=1).to_broadcast([2 * RANK, 1])).then_inc(consts_loaded, 16)
            sp.dma_start(w1_raw[:], w1.rearrange("(c p) d -> p c d", p=P)).then_inc(consts_loaded, 16)
            sp.dma_start(w2_raw[:], w2).then_inc(consts_loaded, 16)
            sp.dma_start(wo_sb[:], wo.rearrange("(q p) n -> p q n", p=P)).then_inc(consts_loaded, 16)

            def run(st):
                if "load" in st.stages:
                    b, par, _ = st.batch(3)
                    if not (isinstance(b, int) and b < 2):
                        wait(sp, xn_made, b - 1)
                        sp.dma_start(x_in[:, par], x_of(b)).then_inc(x_loaded[par], 16)
                if "attn" in st.stages:
                    b, par, _ = st.batch(0)
                    wait(sp, xb2_made, b - 1)
                    sp.dma_start(x_res[:, par], x_of(b)).then_inc(res_loaded[par], 16)
                if "back" in st.stages:
                    b, par, _ = st.batch(-1)
                    wait(sp, y_added, b + 1)
                    sp.dma_start(out[bass.ds(b, 1)].rearrange("o (t p) d -> p (o t) d", p=P),
                                 y_sb[:, par]).then_inc(y_stored[par], 16)

            run_all(sp, run)
            for par in range(2):
                sp.wait_ge(y_stored[par], 16 * (batches // 2))

        @block.tensor
        def _(pe):
            def mm3(o, hi_l, lo_l, hi_r, lo_r, last=True):
                pe.matmul(o, hi_l, hi_r, start=True, stop=False)
                pe.matmul(o, hi_l, lo_r, start=False, stop=False)
                return pe.matmul(o, lo_l, hi_r, start=False, stop=last)

            pe.wait_ge(consts_loaded, 16 * 11)
            pe.wait_ge(ident_made, 2)
            for c in range(HC):
                pe.transpose(ps_scores[:, 0, c * P:(c + 1) * P], w1_raw[:, c], ident[:])
            for c in range(HC):
                pe.transpose(ps_scores[:, 1, c * P:(c + 1) * P], w2_raw[:, c * P:(c + 1) * P], ident[:])
            pe.wait_ge(setup_made, 2)
            pe.transpose(ps_scores[:, 2, 0:PAIRS], g_row[:], ident[0:PAIRS, 0:PAIRS])
            pe.transpose(ps_scores[:, 2, PAIRS:PAIRS + HC], b1_raw[:], ident[0:HC, 0:HC]).then_inc(setup_turned, 1)
            pe.wait_ge(setup_made, 7)

            def aux(st, i, kind, k):
                wait_bank(pe, st, i)
                bank = ps_aux[:, i % AUX_BANKS, :]
                b, par, _ = st.batch(STAGE[kind][1])
                done = aux_filled[kind]
                if kind == "xT":
                    wait(pe, xn_made, b + 1)
                    for t in range(TT):
                        pe.transpose(bank[:, t * P:(t + 1) * P], xh[:, t], ident[:])
                    for t in range(TT):
                        ins = pe.transpose(bank[:, (TT + t) * P:(TT + t + 1) * P], xn[:, par, t], ident[:])
                elif kind == "qk":
                    t, c = k // 4, k % 4
                    if k == 0:
                        wait(pe, xT_split, b + 1)
                    tok, col = slice(t * P, (t + 1) * P), slice(c * 512, (c + 1) * 512)
                    ins = mm3(bank, xhT_hi[:, tok], xhT_lo[:, tok], w_hi[:, col], w_lo[:, col])
                elif kind == "v":
                    t, c = k // 2, k % 2
                    tok, col = slice(t * P, (t + 1) * P), slice(QK + c * 512, QK + (c + 1) * 512)
                    ins = mm3(bank, xhT_hi[:, tok], xhT_lo[:, tok], w_hi[:, col], w_lo[:, col])
                elif kind == "qkT":
                    if k % 2 == 0:
                        wait(pe, qk_normed, 4 * b + k // 2 + 1)
                    for j in range(2):
                        for t in range(TT):
                            at = j * HEADS * DH + k * P
                            ins = pe.transpose(bank[:, (j * TT + t) * P:(j * TT + t + 1) * P],
                                               qk[:, t, at:at + P], ident[:])
                elif kind == "oT":
                    wait(pe, o_normed, PAIRS * b + 2 * k + 2)
                    for j in range(2):
                        for t in range(TT):
                            at = (2 * k + j) * P
                            ins = pe.transpose(bank[:, (j * TT + t) * P:(j * TT + t + 1) * P],
                                               o_sb[:, par, t, at:at + P], ident[:])
                elif kind == "sel":
                    pe.matmul(bank[0:2 * RANK, 0:P], ident[:, 1:4 * RANK:2], xn[:, par, 0], start=True, stop=True)
                    ins = pe.matmul(bank[0:2 * RANK, P:2 * P], ident[:, 2:4 * RANK + 1:2], xn[:, par, 0],
                                    start=True, stop=True)
                elif kind == "low":
                    wait(pe, low_made, 2 * b + k + 1)
                    rows = low1[:].rearrange("p a b -> p (a b)") if k == 0 else low2[:].rearrange("p a b c -> p (a b c)")
                    ins = pe.matmul(bank, sel_rows[:, 1, :], rows, start=True, stop=True)
                elif kind == "hid":
                    if k == 0:
                        wait(pe, weff_made, 2 * b + 1)
                    for j in range(2):
                        ins = pe.matmul(bank[:, j * seq:(j + 1) * seq], w1_eff[:, 2 * k + j], xnT[:, par],
                                        start=True, stop=True)
                ins.then_inc(done, 1)

            def scores(st, h):
                b, par, _ = st.batch(0)
                pair, rows = h // 2, slice(DH * (h % 2), DH * (h % 2) + DH)
                if h % 2 == 0:
                    wait(pe, qkT_split, PAIRS * b + pair + 1)
                wait(pe, clamp_done, HEADS * b + h + 1 - SCORE_BACK[h])
                for t in range(TT):
                    keys = slice(t * P, (t + 1) * P)
                    ins = mm3(ps_scores[:, SCORE_BANK[h], t * seq:(t + 1) * seq],
                              kT_hi[rows, par, pair, keys], kT_lo[rows, par, pair, keys],
                              qT_hi[rows, par, pair], qT_lo[rows, par, pair])
                ins.then_inc(scores_done, 1)

            def values(st, ahead, h):
                b, par, _ = st.batch(ahead)
                pair = h // 2
                if h == 0:
                    wait(pe, v_split, 4 * b + 4)
                if h in POOL_HEADS:
                    wait(pe, lo_by_pool, len(POOL_HEADS) * b + POOL_HEADS.index(h) + 1)
                else:
                    wait(pe, lo_by_vector, vector_count(b, h))
                if h % 2 == 0:
                    wait(pe, o_normed, PAIRS * b + pair - 1)
                buf = h % RING
                hi = probs[:, buf].bitcast(BF16)[:, 1::2]
                for t in range(TT):
                    at = (t * 2 + h % 2) * (DH + 1)
                    full = ps_o[:, pair % 2, at:at + DH + 1]
                    for u in range(TT):
                        col = slice(u * seq + t * P, u * seq + (t + 1) * P)
                        pe.matmul(full, hi[:, col], v_hi[:, par, u, h], start=(u == 0), stop=False)
                        pe.matmul(full[:, 0:DH], hi[:, col], v_lo[:, par, u, h], start=False, stop=False)
                        ins = pe.matmul(full, probs_lo[:, buf, col], v_hi[:, par, u, h],
                                        start=False, stop=(u == TT - 1))
                ins.then_inc(attended, 1)

            def result(st, part):
                b, par, _ = st.batch(-1)
                n = PAIRS + HC
                for j in range(4 * part, 4 * part + 4):
                    t, i = j // n, j % n
                    o = ps_y[:, t * P:(t + 1) * P]
                    if j == 0:
                        wait(pe, y_added, b)
                    if t == 0 and i < PAIRS and i % 2 == 0:
                        wait(pe, oT_copied, 4 * b + i // 2 + 1)
                    if i < PAIRS:
                        ins = pe.matmul(o, oT[:, i, t * P:(t + 1) * P], wo_sb[:, i], start=(i == 0), stop=False)
                    else:
                        c = i - PAIRS
                        ins = pe.matmul(o, hid[:, par, c, t * P:(t + 1) * P], w2_eff[:, par, c],
                                        start=False, stop=(c == HC - 1))
                if part == 2 * n // 4 - 1:
                    ins.then_inc(y_filled, 1)

            def run(st):
                for s in range(HEADS):
                    if "attn" in st.stages:
                        scores(st, s)
                    for i, kind, k in aux_tasks(st, s, PER_BATCH):
                        aux(st, i, kind, k)
                    late = head_of(st, s, 2)
                    if late:
                        values(st, *late)
                    if "back" in st.stages and s in Y_SLOTS:
                        result(st, s - Y_SLOTS[0])

            run_all(pe, run)

        @block.scalar
        def _(act):
            def run(st):
                for s in range(HEADS):
                    if "attn" in st.stages:
                        b, par, _ = st.batch(0)
                        buf = s % RING
                        wait(act, scores_done, HEADS * b + s + 1)
                        wait(act, probs_done, HEADS * b + s + 1 - RING)
                        nc.scalar.activation(clamped[:, buf], ps_scores[:, SCORE_BANK[s]], ACT.Tanh).then_inc(clamp_done, 1)
                    late = head_of(st, s, 1)
                    if late:
                        ahead, h = late
                        b, par, _ = st.batch(ahead)
                        buf = h % RING
                        wait(act, clamp_done, HEADS * b + h + 1)
                        wait(act, attended, HEADS * b + h + 1 - RING)
                        nc.scalar.activation(probs[:, buf], clamped[:, buf], ACT.Exp, bias=lift_col[:, 0:1],
                                             scale=SOFTCLAMP * DH ** -0.5).then_inc(probs_done, 1)
                    for i, kind, k in aux_tasks(st, s, ("xT", "qk", "v", "oT", "qkT", "hid")):
                        b, par, _ = st.batch(STAGE[kind][1])
                        bank = ps_aux[:, i % AUX_BANKS, :]
                        act.wait_ge(aux_filled[kind], PER_BATCH[kind] * b + k + 1)
                        if kind == "xT":
                            nc.scalar.copy(xnT[:, par], bank[:, seq:2 * seq])
                            nc.scalar.copy(xhT_hi[:], bank[:, 0:seq]).then_inc(xT_hi_made, 1)
                        elif kind == "qk":
                            if k == 0:
                                wait(act, aux_filled["qkT"], PAIRS * b)
                            t, c = k // 4, k % 4
                            nc.scalar.copy(qk[:, t, c * 512:(c + 1) * 512], bank).then_inc(qk_copied, 1)
                        elif kind == "v":
                            if k == 0:
                                wait(act, attended, HEADS * (b - 1))
                            t, c = k // 2, k % 2
                            nc.scalar.copy(v_hi[:, par, t, 8 * c:8 * c + 8, 0:DH],
                                           bank.rearrange("p (h d) -> p h d", d=DH)).then_inc(v_hi_made, 1)
                        elif kind == "oT":
                            nc.scalar.copy(oT[:, 2 * k:2 * k + 2], bank.rearrange("p (j t) -> p j t", j=2))\
                                .then_inc(oT_copied, 1)
                        elif kind == "qkT":
                            nc.scalar.activation(qT_hi[:, par, k], bank[:, 0:seq], ACT.Copy, scale=g_col[:, k:k + 1])
                            nc.scalar.copy(kT_hi[:, par, k], bank[:, seq:2 * seq]).then_inc(qkT_hi_made, 1)
                        elif kind == "hid":
                            for j in range(2):
                                c = 2 * k + j
                                nc.scalar.activation(hid[:, par, c], bank[:, j * seq:(j + 1) * seq], ACT.Gelu,
                                                     bias=b1_col[:, c:c + 1]).then_inc(gelu_done, 1)

            act.wait_ge(setup_made, 7)
            run_all(act, run)

        @block.vector
        def _(dve):
            v = nc.vector
            v.memset(v_hi[:, :, :, :, DH:DH + 1], 1.0)
            v.memset(lift_col[:], LIFT)
            dve.wait_ge(consts_loaded, 16 * 11)
            v.tensor_scalar(g_raw[:], g_raw[:], 1.0, None, ALU.add).then_inc(setup_made, 1)
            dve.wait_ge(setup_made, 1)
            v.scalar_tensor_tensor(g_row[:], g_raw[:, 0], DH / SOFTCLAMP, g_raw[:, 1],
                                   ALU.mult, ALU.mult).then_inc(setup_made, 1)
            v.tensor_scalar(w_raw[:], w_raw[:], nw_col[:, 0:1], None, ALU.mult).then_inc(setup_made, 1)
            dve.wait_ge(setup_made, 3)
            v.tensor_copy(w_hi[:], w_raw[:]).then_inc(setup_made, 1)
            dve.wait_ge(setup_made, 4)
            v.tensor_tensor(w_lo[:], w_raw[:], w_hi[:].bitcast(F32), ALU.subtract).then_inc(setup_made, 1)
            dve.wait_ge(setup_turned, 1)
            v.tensor_copy(g_col[:], ps_scores[:, 2, 0:PAIRS])
            v.tensor_copy(b1_col[:], ps_scores[:, 2, PAIRS:PAIRS + HC])
            v.tensor_copy(w1T[:].rearrange("p a b -> p (a b)"), ps_scores[:, 0]).then_inc(setup_made, 1)
            v.tensor_copy(w2T[:].rearrange("p a b -> p (a b)"), ps_scores[:, 1]).then_inc(setup_made, 1)
            dve.wait_ge(masks_made, 2)
            m1, m2 = mask1[:].rearrange("p a b -> p (a b)"), mask2[:].rearrange("p a b c -> p (a b c)")
            v.tensor_scalar(m1, m1, scale_col[:, 0:1], None, ALU.mult).then_inc(setup_made, 1)
            v.tensor_scalar(m2, m2, scale_col[:, 0:1], None, ALU.mult).then_inc(setup_made, 1)
            dve.wait_ge(setup_made, 9)

            def norm_stats(st):
                b, par, half = st.batch(2)
                dve.wait_ge(x_loaded[par], 16 * (half + 1))
                for t in range(TT):
                    v.bn_stats(stats[:, t], x_in[:, par, t]).then_inc(stats_made, 1)

            def norm_var(st):
                b, par, _ = st.batch(2)
                dve.wait_ge(stats_made, 2 * b + 2)
                v.memset(scratch[:], 0.0)
                for t in range(TT):
                    v.bn_aggr(mean_var[:, t], stats[:, t]).then_inc(meanvar_made, 1)

            def norm_eps(st):
                b, par, _ = st.batch(2)
                dve.wait_ge(meanvar_made, 2 * b + 2)
                v.tensor_scalar(var_eps[:, 0], mean_var[:, :, 1], LN_EPS, None, ALU.add).then_inc(vareps_made, 1)
                v.tensor_scalar(var_eps[:, 1], mean_var[:, :, 1], 1.0 + RMS_EPS, RMS_EPS * LN_EPS,
                                ALU.mult, ALU.add).then_inc(vareps_made, 1)

            def norm_apply(st):
                b, par, _ = st.batch(2)
                dve.wait_ge(rstd_made, b + 1)
                wait(dve, aux_filled["xT"], b)
                wait(dve, aux_filled["sel"], b - 1)
                for j in range(2):
                    for t in range(TT):
                        o = xn[:, par, t] if j == 0 else xh[:, t]
                        ins = v.tensor_scalar(o, x_in[:, par, t], mean_var[:, t, 0:1], rstd[:, j, t:t + 1],
                                              ALU.subtract, ALU.mult)
                ins.then_inc(xn_made, 1)

            def xT_lo(st, bank):
                b, _, _ = st.batch(1)
                dve.wait_ge(xT_hi_made, b + 1)
                v.tensor_tensor(xhT_lo[:], bank[:, 0:seq], xhT_hi[:].bitcast(F32), ALU.subtract).then_inc(xT_split, 1)

            def sum_squares(st, k):
                b, _, _ = st.batch(1)
                dve.wait_ge(sq_made, 8 * b + k + 1)
                v.tensor_reduce(norm2[:, 8 * k:8 * k + 8], sq[:, k % 2].rearrange("p (h d) -> p h d", d=DH),
                                AX_X, ALU.add).then_inc(norm2_made, 1)

            def rsqrt_safe(st):
                b, _, _ = st.batch(1)
                dve.wait_ge(norm2_made, 8 * b + 8)
                v.tensor_scalar(norm2_safe[:], norm2[:], NORM2_MIN, None, ALU.max).then_inc(seed_made, 1)

            def rsqrt_seed(st):
                b, _, _ = st.batch(1)
                dve.wait_ge(seed_made, 3 * b + 1)
                wait(dve, qk_normed, 4 * b)
                v.tensor_scalar(minus_half_norm2[:], norm2_safe[:], -0.5, None, ALU.mult).then_inc(seed_made, 1)
                v.tensor_scalar(rnorm[:].bitcast(I32), norm2_safe[:].bitcast(I32), -0.5, RSQRT_SEED,
                                ALU.mult, ALU.add).then_inc(seed_made, 1)

            def normalise(st, c):
                b, _, _ = st.batch(1)
                if c == 0:
                    dve.wait_ge(newton_step, 12 * b + 12)
                    dve.wait_ge(sq_made, 8 * b + 8)
                part = qk[:].rearrange("p t (j n) -> p (t j) n", j=2)[:, :, c * 4 * DH:(c + 1) * 4 * DH]\
                    .rearrange("p a (h d) -> p a h d", d=DH)
                r = rnorm[:].rearrange("p (a h) -> p a h", h=HEADS)[:, :, 4 * c:4 * c + 4]
                v.tensor_tensor(part, part, r.unsqueeze(3).to_broadcast([P, 2 * TT, 4, DH]), ALU.mult)\
                    .then_inc(qk_normed, 1)

            def lo_part(st, ahead, h):
                b, _, _ = st.batch(ahead)
                buf = h % RING
                dve.wait_ge(probs_done, HEADS * b + h + 1)
                v.tensor_tensor(probs_lo[:, buf], probs[:, buf], probs[:, buf].bitcast(BF16)[:, 1::2], ALU.subtract)\
                    .then_inc(lo_by_vector, 1)

            def divide(st, ahead, pair):
                b, par, _ = st.batch(ahead)
                got = ps_o[:, pair % 2, 0:4 * (DH + 1)].rearrange("p (a d) -> p a d", d=DH + 1)
                dve.wait_ge(attended, HEADS * b + 2 * pair + 2)
                v.reciprocal(rden[:, pair % 2], got[:, :, DH]).then_inc(rden_made, 1)
                dve.wait_ge(rden_made, PAIRS * b + pair + 1)
                if pair == 0:
                    wait(dve, aux_filled["oT"], 4 * (b - 1))
                v.tensor_tensor(o_sb[:, par, :, pair * P:(pair + 1) * P].rearrange("p t (j d) -> p t j d", d=DH),
                                got[:, :, 0:DH].rearrange("p (t j) d -> p t j d", j=2),
                                rden[:, pair % 2].rearrange("p (t j) -> p t j", j=2).unsqueeze(3)
                                .to_broadcast([P, TT, 2, DH]), ALU.mult).then_inc(o_normed, 1)

            def result(st):
                b, par, half = st.batch(-1)
                dve.wait_ge(y_filled, b + 1)
                dve.wait_ge(xb2_made, b + 1)
                wait(dve, y_stored[par], 16 * half)
                v.tensor_tensor(y_sb[:, par].rearrange("p t d -> p (t d)"), ps_y[:, 0:seq],
                                x_b2[:].rearrange("p t d -> p (t d)"), ALU.add).then_inc(y_added, 1)

            def aux(st, i, kind, k):
                b, par, _ = st.batch(STAGE[kind][1])
                bank = ps_aux[:, i % AUX_BANKS, :]
                if kind == "xT":
                    xT_lo(st, bank)
                elif kind == "v":
                    dve.wait_ge(v_hi_made, 4 * b + k + 1)
                    t, c = k // 2, k % 2
                    v.tensor_tensor(v_lo[:, par, t, 8 * c:8 * c + 8], bank.rearrange("p (h d) -> p h d", d=DH),
                                    v_hi[:, par, t, 8 * c:8 * c + 8, 0:DH], ALU.subtract).then_inc(v_split, 1)
                elif kind == "qkT":
                    dve.wait_ge(qkT_hi_made, PAIRS * b + k + 1)
                    v.scalar_tensor_tensor(qT_lo[:, par, k], bank[:, 0:seq], g_col[:, k:k + 1], qT_hi[:, par, k],
                                           ALU.mult, ALU.subtract)
                    v.tensor_tensor(kT_lo[:, par, k], bank[:, seq:2 * seq], kT_hi[:, par, k], ALU.subtract)\
                        .then_inc(qkT_split, 1)
                elif kind == "sel":
                    dve.wait_ge(aux_filled["sel"], b + 1)
                    wait(dve, aux_filled["low"], 2 * b)
                    v.tensor_copy(sel_rows[:].rearrange("p a b -> p (a b)"), bank[0:2 * RANK, 0:2 * P])\
                        .then_inc(sel_copied, 1)
                    dve.wait_ge(sel_copied, b + 1)
                    even = sel_rows[:, 0]
                    v.tensor_tensor(low1[:], even.unsqueeze(1).to_broadcast([2 * RANK, RANK, P]), mask1[:], ALU.mult)\
                        .then_inc(low_made, 1)
                    v.tensor_tensor(low2[:], even.rearrange("p (o t) -> p t o", t=HC).unsqueeze(2)
                                    .to_broadcast([2 * RANK, HC, RANK, P // RANK]), mask2[:], ALU.mult)\
                        .then_inc(low_made, 1)
                elif kind == "low":
                    dve.wait_ge(aux_filled["low"], 2 * b + k + 1)
                    if k == 1:
                        wait(dve, y_filled, b - 1)
                    o, base = (w1_eff[:], w1T) if k == 0 else (w2_eff[:, par], w2T)
                    v.tensor_tensor(o, bank.rearrange("p (c n) -> p c n", c=HC), base[:], ALU.add)\
                        .then_inc(weff_made, 1)

            def run(st):
                for s in range(HEADS):
                    late = head_of(st, s, 1)
                    if late and late[1] not in POOL_HEADS:
                        lo_part(st, *late)
                    late = head_of(st, s, 3)
                    if late and late[1] % 2 == 1:
                        divide(st, late[0], late[1] // 2)
                    for i, kind, k in aux_tasks(st, s, ("xT", "v", "qkT", "sel", "low")):
                        aux(st, i, kind, k)
                    if "front" in st.stages:
                        if 2 <= s < 6:
                            sum_squares(st, 2 * s - 4)
                            sum_squares(st, 2 * s - 3)
                        if s == 6:
                            rsqrt_safe(st)
                            rsqrt_seed(st)
                        if 9 <= s < 13:
                            normalise(st, s - 9)
                    if "norm" in st.stages:
                        if s == 10:
                            norm_stats(st)
                        if s == 11:
                            norm_var(st)
                            norm_eps(st)
                        if s == 14:
                            norm_apply(st)
                    if "back" in st.stages and s == HEADS - 1:
                        result(st)

            run_all(dve, run)

        @block.gpsimd
        def _(pool):
            g = nc.gpsimd
            g.memset(minus_half[:], -0.5)
            g.memset(newton_c[:], 1.5)
            g.memset(mask1[:], 0.0)
            g.memset(mask2[:], 0.0)
            g.memset(ident[:], 0.0).then_inc(ident_made, 1)
            pool.wait_ge(ident_made, 1)
            g.affine_select(out=ident[:], in_=ident[:], compare_op=ALU.not_equal, fill=1.0, base=0,
                            pattern=[[-1, P]], channel_multiplier=1).then_inc(ident_made, 1)
            g.affine_select(out=mask1[:], in_=mask1[:], compare_op=ALU.not_equal, fill=1.0, base=0,
                            pattern=[[-1, RANK], [0, P]], channel_multiplier=1).then_inc(masks_made, 1)
            g.affine_select(out=mask2[:], in_=mask2[:], compare_op=ALU.not_equal, fill=1.0, base=-RANK,
                            pattern=[[0, HC], [-1, RANK], [0, P // RANK]], channel_multiplier=1)\
                .then_inc(masks_made, 1)

            def square(st, k):
                b, _, _ = st.batch(1)
                t, c = k // 4, k % 4
                part = qk[:, t, c * 512:(c + 1) * 512]
                pool.wait_ge(qk_copied, 8 * b + k + 1)
                wait(pool, norm2_made, 8 * b + k - 1)
                g.tensor_tensor(sq[:, k % 2], part, part, ALU.mult).then_inc(sq_made, 1)

            def newton(st, turn):
                b, _, _ = st.batch(1)
                if turn == 0:
                    pool.wait_ge(seed_made, 3 * b + 3)
                n = 12 * b + 4 * turn

                def after(k):
                    wait(pool, newton_step, n + k)

                after(0)
                g.tensor_tensor(newton_a[:], rnorm[:], rnorm[:], ALU.mult).then_inc(newton_step, 1)
                after(1)
                g.tensor_tensor(newton_b[:], newton_a[:], minus_half_norm2[:], ALU.mult).then_inc(newton_step, 1)
                after(2)
                g.tensor_tensor(newton_a[:], newton_b[:], newton_c[:], ALU.add).then_inc(newton_step, 1)
                after(3)
                g.tensor_tensor(rnorm[:], rnorm[:], newton_a[:], ALU.mult).then_inc(newton_step, 1)

            def run(st):
                for s in range(HEADS):
                    late = head_of(st, s, 1)
                    if late and late[1] in POOL_HEADS:
                        ahead, h = late
                        b, _, _ = st.batch(ahead)
                        buf = h % RING
                        pool.wait_ge(probs_done, HEADS * b + h + 1)
                        g.tensor_tensor(probs_lo[:, buf], probs[:, buf], probs[:, buf].bitcast(BF16)[:, 1::2],
                                        ALU.subtract).then_inc(lo_by_pool, 1)
                    if "front" in st.stages:
                        if 1 <= s < 5:
                            square(st, 2 * s - 2)
                            square(st, 2 * s - 1)
                        if 6 <= s < 9:
                            newton(st, s - 6)
                    if "back" in st.stages and s == 9:
                        b, par, half = st.batch(-1)
                        pool.wait_ge(res_loaded[par], 16 * (half + 1))
                        wait(pool, y_added, b)
                        g.tensor_tensor(x_b2[:], x_res[:, par], b2_bc[:].unsqueeze(1).to_broadcast([P, TT, P]),
                                        ALU.add).then_inc(xb2_made, 1)
                    if "norm" in st.stages and s == 12:
                        b, _, _ = st.batch(2)
                        pool.wait_ge(vareps_made, 2 * b + 2)
                        wait(pool, xn_made, b)
                        g.tensor_tensor(rstd[:].rearrange("p a b -> p (a b)"),
                                        var_eps[:].rearrange("p a b -> p (a b)"), minus_half[:], ALU.pow)\
                            .then_inc(rstd_made, 1)

            pool.wait_ge(consts_loaded, 16 * 11)
            run_all(pool, run)


_INS = ["L0_attn_tokens", "L0_attn_norm_w", "L0_attn_Wq", "L0_attn_Wkv", "L0_attn_Wo", "L0_attn_q_gamma",
        "L0_attn_k_gamma", "L0_ffn_W1", "L0_ffn_b1", "L0_ffn_W2", "L0_ffn_b2", "L0_ffn_scale"]


def kernel(**inputs):
    import numpy as _np
    import concourse.bacc as _bacc
    from concourse import mybir as _mybir
    from concourse.bass_utils import run_bass_kernel_spmd as _run

    nc = _bacc.Bacc("TRN2", target_bir_lowering=False, num_devices=1)
    arrays, args = {}, []
    for name in _INS:
        a = _np.ascontiguousarray(inputs[name])
        if a.ndim == 0:
            a = a.reshape(1)
        arrays[f"in_{name}_dram"] = a
        args.append(nc.dram_tensor(f"in_{name}_dram", a.shape, _mybir.dt.from_np(a.dtype), kind="ExternalInput").ap())
    shape = tuple(inputs["L0_attn_tokens"].shape)
    out = nc.dram_tensor("out_0_dram", shape, _mybir.dt.float32, kind="ExternalOutput").ap()
    block_kernel(nc, *args, out)
    r = _run(nc, [arrays], core_ids=[0])
    return r.results[0]["out_0_dram"]
```

```python
from contextlib import ExitStack

import concourse.bass as bass
from concourse import mybir

F32 = mybir.dt.float32
F32R = mybir.dt.float32r
BF16 = mybir.dt.bfloat16
F16 = mybir.dt.float16
I32 = mybir.dt.int32
ALU = mybir.AluOpType
ACT = mybir.ActivationFunctionType
AX_X = mybir.AxisListType.X

P = 128
HEADS = 16
DH = 64
PAIRS = HEADS // 2
HIDDEN = 512
HC = HIDDEN // P
RANK = 4
SOFTCLAMP = 50.0
LN_EPS = 1e-5
RMS_EPS = 2.0 ** -23
NORM2_MIN = 1e-24
RSQRT_SEED = float(0x5F3759DF)
LIFT = 4.1588830833596715

AUX_BANKS = 3
AUX = [
    (0, "sel", 0, 0), (0, "qk", 0, 1),
    (1, "qk", 1, 1), (1, "qk", 2, 1),
    (2, "qk", 3, 1), (2, "qk", 4, 1),
    (3, "qk", 5, 1), (3, "qk", 6, 1),
    (4, "qk", 7, 1), (4, "qkT", 4, 0),
    (5, "qkT", 5, 0), (5, "low", 0, 0),
    (6, "low", 1, 0), (6, "oT", 0, -1),
    (7, "oT", 1, -1), (7, "oT", 2, -1),
    (8, "qkT", 6, 0), (8, "oT", 3, -1),
    (9, "hid", 0, 0), (9, "hid", 1, 0),
    (10, "qkT", 7, 0),
    (11, "v", 0, 1),
    (12, "v", 1, 1), (12, "qkT", 0, 1),
    (13, "v", 2, 1), (13, "xT", 0, 2),
    (14, "v", 3, 1), (14, "qkT", 1, 1),
    (15, "qkT", 2, 1), (15, "qkT", 3, 1),
]
assert len(AUX) % AUX_BANKS == 0
PER_BATCH = {"xT": 1, "qk": 8, "v": 4, "oT": 4, "sel": 1, "low": 2, "qkT": 8, "hid": 2}
STAGE = {2: "norm", 1: "front", 0: "attn", -1: "back"}
SCORE_BANKS = 2
RING = 4
VALUES_LAG = 3
POOL_HEADS = (8, 10, 11, 13, 14)
SQUARES = {0: (0,), 1: (1,), 2: (2, 3), 3: (4,), 4: (5,), 5: (6, 7)}
SUMS = {1: (0,), 2: (1,), 3: (2, 3), 4: (4,), 5: (5,), 6: (6, 7)}
SCALES = {1: (0,), 4: (4,), 10: (1, 5)}
NEWTON = {7: (0, 1), 8: (2,)}
NORMALISE = (10, 11, 13, 14)
Y_PRODUCTS = {2: 2, 4: 1, 5: 1, 7: 2, 8: 2, 10: 4, 11: 4, 12: 2, 13: 2, 14: 2, 15: 2}


class Step:

    def __init__(self, half, odd, stages):
        self.half, self.odd, self.stages = half, odd, stages

    def batch(self, ahead):
        m = self.odd + ahead
        return 2 * self.half + m, m % 2, self.half + m // 2


def stages_of(n, batches):
    out = set()
    if 0 <= n < batches:
        out.add("attn")
    if 0 <= n + 1 < batches:
        out.add("front")
    if 0 <= n + 2 < batches:
        out.add("norm")
    if 0 <= n + 3 < batches:
        out.add("load")
    if 0 <= n - 1 < batches:
        out.add("back")
    if 0 <= n - 2 < batches:
        out.add("store")
    return out


def block_kernel(nc, tokens, norm_w, wq, wkv, wo, q_gamma, k_gamma, w1, b1, w2, b2, scale, out):
    batches, seq, dim = tokens.shape
    TT = seq // P
    assert dim == P and TT == 2 and wq.shape[1] == HEADS * DH and w1.shape[0] == HIDDEN and batches % 2 == 0
    QK = 2 * HEADS * DH
    QKV = QK + HEADS * DH

    with ExitStack() as ctx:
        def sb(name, shape, dt=F32):
            return ctx.enter_context(nc.sbuf_tensor(name, shape, dt))

        def sem(name):
            return ctx.enter_context(nc.semaphore(name))

        ps_scores = ctx.enter_context(nc.psum_tensor("ps_scores", [P, SCORE_BANKS, 512], F32))
        ps_o = ctx.enter_context(nc.psum_tensor("ps_o", [P, 2, 512], F32))
        ps_aux = ctx.enter_context(nc.psum_tensor("ps_aux", [P, AUX_BANKS, 512], F32))
        ps_y = ctx.enter_context(nc.psum_tensor("ps_y", [P, 512], F32))

        ident = sb("ident", [P, P])
        w_hi = sb("w_hi", [P, QKV], F32R)
        w_lo = sb("w_lo", [P, QKV], F32R)
        wo_sb = sb("wo_sb", [P, PAIRS, P])
        w1T = sb("w1T", [P, HC, P])
        w2T = sb("w2T", [P, HC, P])
        nw_col = sb("nw_col", [P, 1])
        g_bc = sb("g_bc", [P, HEADS * DH])
        b1_raw = sb("b1_raw", [HC, P])
        b1_col = sb("b1_col", [P, HC])
        b2_bc = sb("b2_bc", [P, P])
        scale_col = sb("scale_col", [2 * RANK, 1])
        mask1 = sb("mask1", [2 * RANK, RANK, P])
        mask2 = sb("mask2", [2 * RANK, HC, RANK, P // RANK])
        minus_half = sb("minus_half", [P, 4])
        scratch = sb("scratch", [P, 1])
        newton_c = sb("newton_c", [P, TT * 2 * HEADS])

        x_in = sb("x_in", [P, 2, TT, P])
        x_res = sb("x_res", [P, 2, TT, P])
        x_b2 = sb("x_b2", [P, TT, P])
        stats = sb("stats", [P, TT, 6])
        mean_var = sb("mean_var", [P, TT, 2])
        var_eps = sb("var_eps", [P, 2, TT])
        rstd = sb("rstd", [P, 2, TT])
        xn = sb("xn", [P, 2, TT, P])
        xh = sb("xh", [P, TT, P])
        xnT = sb("xnT", [P, 2, seq])
        xhT_hi = sb("xhT_hi", [P, 2, seq], F32R)
        xhT_lo = sb("xhT_lo", [P, 2, seq], F32R)
        qk = sb("qk", [P, 2, TT, QK])
        early = qk[:, 1].rearrange("p t n -> p (t n)")
        w_raw = early[:, 0:QKV]
        w1_raw = early[:, QKV:QKV + HIDDEN].rearrange("p (c n) -> p c n", c=HC)
        w2_raw = early[:, QKV + HIDDEN:QKV + 2 * HIDDEN]
        sq = sb("sq", [P, 2, 512])
        norm2 = sb("norm2", [P, TT * 2 * HEADS])
        norm2_safe = sb("norm2_safe", [P, TT * 2 * HEADS])
        minus_half_norm2 = sb("minus_half_norm2", [P, TT * 2 * HEADS])
        rnorm = sb("rnorm", [P, TT * 2 * HEADS])
        newton_a = sb("newton_a", [P, TT * 2 * HEADS])
        newton_b = sb("newton_b", [P, TT * 2 * HEADS])
        heads_T = sb("heads_T", [P, PAIRS, 3, 2, seq], F16)
        v_hi = sb("v_hi", [P, 2, TT, HEADS, DH + 1], BF16)
        v_lo = sb("v_lo", [P, 2, TT, HEADS, DH], BF16)
        clamped = sb("clamped", [P, RING, TT * seq])
        probs = sb("probs", [P, RING, TT * seq])
        probs_lo = sb("probs_lo", [P, RING, TT * seq], F16)
        rden = sb("rden", [P, 2, 4])
        o_sb = sb("o_sb", [P, 2, TT, HEADS * DH])
        oT = sb("oT", [P, PAIRS, seq])
        sel_rows = sb("sel_rows", [2 * RANK, 2, P])
        low1 = sb("low1", [2 * RANK, RANK, P])
        low2 = sb("low2", [2 * RANK, HC, RANK, P // RANK])
        w1_eff = sb("w1_eff", [P, HC, P])
        w2_eff = sb("w2_eff", [P, 2, HC, P])
        hid = sb("hid", [P, 2, HC, seq])
        g_raw = hid[:].rearrange("p a c t -> p a (c t)")
        y_sb = sb("y_sb", [P, 2, TT, P])

        consts_loaded = sem("consts_loaded")
        ident_made = sem("ident_made")
        masks_made = sem("masks_made")
        setup_made = sem("setup_made")
        setup_turned = sem("setup_turned")
        x_loaded = [sem(f"x_loaded{i}") for i in range(2)]
        res_loaded = [sem(f"res_loaded{i}") for i in range(2)]
        y_stored = [sem(f"y_stored{i}") for i in range(2)]
        stats_made = sem("stats_made")
        meanvar_made = sem("meanvar_made")
        vareps_made = sem("vareps_made")
        rstd_made = sem("rstd_made")
        xn_made = sem("xn_made")
        sq_made = sem("sq_made")
        norm2_made = sem("norm2_made")
        seed_made = sem("seed_made")
        newton_step = sem("newton_step")
        q_scaled = sem("q_scaled")
        qk_normed = sem("qk_normed")
        scores_done = sem("scores_done")
        clamp_done = sem("clamp_done")
        probs_done = sem("probs_done")
        lo_by_vector = sem("lo_by_vector")
        lo_by_pool = sem("lo_by_pool")
        attended = sem("attended")
        rden_made = sem("rden_made")
        o_normed = sem("o_normed")
        aux_filled = {k: sem(f"{k}_filled") for k in PER_BATCH}
        xT_hi_made = sem("xT_hi_made")
        xT_split = sem("xT_split")
        qk_copied = sem("qk_copied")
        v_hi_made = sem("v_hi_made")
        v_split = sem("v_split")
        qkT_hi_made = sem("qkT_hi_made")
        qkT_split = sem("qkT_split")
        second_moved = sem("second_moved")
        crossed = [sem(f"crossed{i}") for i in range(2)]
        oT_copied = sem("oT_copied")
        sel_copied = sem("sel_copied")
        low_made = sem("low_made")
        weff_made = sem("weff_made")
        gelu_done = sem("gelu_done")
        y_filled = sem("y_filled")
        xb2_made = sem("xb2_made")
        y_added = sem("y_added")

        AUX_READ = {"xT": (xT_split, 1), "qk": (qk_copied, 1), "v": (v_split, 1), "qkT": (qkT_split, 1),
                    "oT": (oT_copied, 1), "sel": (sel_copied, 1), "low": (weff_made, 1), "hid": (gelu_done, 2)}

        def wait(eng, s, value):
            if isinstance(value, int) and value <= 0:
                return
            eng.wait_ge(s, value)

        def wait_bank(eng, st, index):
            for back in range(1, 3 * len(AUX)):
                i = index - back * AUX_BANKS
                rounds, j = i // len(AUX), i % len(AUX)
                if rounds < -1:
                    return
                _, kind, k, ahead = AUX[j]
                if STAGE[ahead] in (st.stages if rounds == 0 else st.before):
                    s, per = AUX_READ[kind]
                    wait(eng, s, per * PER_BATCH[kind] * st.batch(ahead + rounds)[0] + per * (k + 1))
                    return

        def aux_tasks(st, slot, kinds):
            for i, (s, kind, k, ahead) in enumerate(AUX):
                if s == slot and kind in kinds and STAGE[ahead] in st.stages:
                    yield i, kind, k, ahead

        def head_of(st, slot, lag):
            ahead, head = (0, slot - lag) if slot >= lag else (-1, slot - lag + HEADS)
            there = "attn" if ahead == 0 else "back"
            return (ahead, head) if there in st.stages else None

        def plan(run):
            def straight(n):
                st = Step(n // 2, n % 2, stages_of(n, batches))
                st.before = stages_of(n - 1, batches)
                run(st)

            first, last = 3, batches - 4
            for n in range(-2, first):
                straight(n)
            yield first // 2, (last + 1) // 2
            for n in range(last + 1, batches + 2):
                straight(n)

        def run_all(eng, run):
            for start, end in plan(run):
                with eng.Fori(start, end) as i:
                    for odd in (1, 2):
                        st = Step(i, odd, stages_of(3, batches))
                        st.before = st.stages
                        run(st)

        def vector_count(b, h):
            return (HEADS - len(POOL_HEADS)) * b + len([i for i in range(h + 1) if i not in POOL_HEADS])

        block = ctx.enter_context(nc.Block())

        @block.sync
        def _(sp):
            def x_of(b):
                return tokens[bass.ds(b, 1)].rearrange("o (t p) d -> p (o t) d", p=P)

            sp.dma_start(x_in[:, 0], tokens[0].rearrange("(t p) d -> p t d", p=P)).then_inc(x_loaded[0], 16)
            sp.dma_start(x_in[:, 1], tokens[1].rearrange("(t p) d -> p t d", p=P)).then_inc(x_loaded[1], 16)
            sp.dma_start(nw_col[:], norm_w.rearrange("(p o) -> p o", o=1)).then_inc(consts_loaded, 16)
            sp.dma_start(w_raw[:, 0:HEADS * DH], wq).then_inc(consts_loaded, 16)
            sp.dma_start(w_raw[:, HEADS * DH:QKV], wkv).then_inc(consts_loaded, 16)
            for j, gamma in enumerate((q_gamma, k_gamma)):
                sp.dma_start(g_raw[:, j], gamma.rearrange("(o h) d -> o (h d)", o=1).to_broadcast([P, HEADS * DH]))\
                    .then_inc(consts_loaded, 16)
            sp.dma_start(b1_raw[:], b1.rearrange("(c p) -> c p", p=P)).then_inc(consts_loaded, 16)
            sp.dma_start(b2_bc[:], b2.rearrange("(o d) -> o d", o=1).to_broadcast([P, P])).then_inc(consts_loaded, 16)
            sp.dma_start(scale_col[:], scale.rearrange("(o d) -> o d", o=1).to_broadcast([2 * RANK, 1])).then_inc(consts_loaded, 16)
            sp.dma_start(w1_raw, w1.rearrange("(c p) d -> p c d", p=P)).then_inc(consts_loaded, 16)
            sp.dma_start(w2_raw, w2).then_inc(consts_loaded, 16)
            sp.dma_start(wo_sb[:], wo.rearrange("(q p) n -> p q n", p=P)).then_inc(consts_loaded, 16)

            def spread(st, k, ahead):
                b, _, _ = st.batch(ahead)
                pair = heads_T[:, k].rearrange("p a j t -> p (a j) t")
                here, moved, before = [v if isinstance(v, int) else sp.to_reg(v) for v in (
                    PAIRS * b + k + 1, 16 * (PAIRS * b + k + 1), 32 * (PAIRS // 2 * b + k // 2))]
                sp.wait_ge(qkT_hi_made, here)
                sp.dma_start(pair[DH:P, 2:4], pair[DH:P, 0:2]).then_inc(second_moved, 16)
                sp.wait_ge(qkT_split, here)
                sp.wait_ge(second_moved, moved)
                wait(sp, crossed[k % 2], before)
                sp.dma_start(pair[DH:P, 0:2], pair[0:DH, 0:6:5]).then_inc(crossed[k % 2], 16)
                sp.dma_start(pair[0:DH, 2:4], pair[DH:P, 2:6:3]).then_inc(crossed[k % 2], 16)

            def run(st):
                if "load" in st.stages:
                    b, par, _ = st.batch(3)
                    if not (isinstance(b, int) and b < 2):
                        wait(sp, xn_made, b - 1)
                        sp.dma_start(x_in[:, par], x_of(b)).then_inc(x_loaded[par], 16)
                if "attn" in st.stages:
                    b, par, _ = st.batch(0)
                    wait(sp, xb2_made, b - 1)
                    sp.dma_start(x_res[:, par], x_of(b)).then_inc(res_loaded[par], 16)
                if "store" in st.stages:
                    b, par, _ = st.batch(-2)
                    wait(sp, y_added, b + 1)
                    sp.dma_start(out[bass.ds(b, 1)].rearrange("o (t p) d -> p (o t) d", p=P),
                                 y_sb[:, par]).then_inc(y_stored[par], 16)
                for s in range(HEADS):
                    for _, _, k, ahead in aux_tasks(st, s, ("qkT",)):
                        spread(st, k, ahead)

            run_all(sp, run)
            for par in range(2):
                sp.wait_ge(y_stored[par], 16 * (batches // 2))

        @block.tensor
        def _(pe):
            def mm3(o, hi_l, lo_l, hi_r, lo_r, last=True):
                pe.matmul(o, hi_l, hi_r, start=True, stop=False)
                pe.matmul(o, hi_l, lo_r, start=False, stop=False)
                return pe.matmul(o, lo_l, hi_r, start=False, stop=last)

            pe.wait_ge(consts_loaded, 16 * 11)
            pe.wait_ge(ident_made, 2)
            for c in range(HC):
                pe.transpose(ps_aux[:, 0, c * P:(c + 1) * P], w1_raw[:, c], ident[:])
            for c in range(HC):
                pe.transpose(ps_aux[:, 1, c * P:(c + 1) * P], w2_raw[:, c * P:(c + 1) * P], ident[:])
            pe.transpose(ps_aux[:, 2, 0:HC], b1_raw[:], ident[0:HC, 0:HC]).then_inc(setup_turned, 1)
            pe.wait_ge(setup_made, 8)

            def aux(st, i, kind, k, ahead):
                wait_bank(pe, st, i)
                bank = ps_aux[:, i % AUX_BANKS, :]
                b, par, _ = st.batch(ahead)
                done = aux_filled[kind]
                if kind == "xT":
                    wait(pe, xn_made, b + 1)
                    for t in range(TT):
                        pe.transpose(bank[:, t * P:(t + 1) * P], xh[:, t], ident[:])
                    for t in range(TT):
                        ins = pe.transpose(bank[:, (TT + t) * P:(TT + t + 1) * P], xn[:, par, t], ident[:])
                elif kind == "qk":
                    t, c = k // 4, k % 4
                    if k == 0:
                        wait(pe, xT_split, b + 1)
                    tok, col = slice(t * P, (t + 1) * P), slice(c * 512, (c + 1) * 512)
                    ins = mm3(bank, xhT_hi[:, par, tok], xhT_lo[:, par, tok], w_hi[:, col], w_lo[:, col])
                elif kind == "v":
                    t, c = k // 2, k % 2
                    tok, col = slice(t * P, (t + 1) * P), slice(QK + c * 512, QK + (c + 1) * 512)
                    ins = mm3(bank, xhT_hi[:, par, tok], xhT_lo[:, par, tok], w_hi[:, col], w_lo[:, col])
                elif kind == "qkT":
                    if k % 2 == 0:
                        wait(pe, qk_normed, 4 * b + k // 2 + 1)
                    for j in range(2):
                        for t in range(TT):
                            at = j * HEADS * DH + k * P
                            ins = pe.transpose(bank[:, (j * TT + t) * P:(j * TT + t + 1) * P],
                                               qk[:, par, t, at:at + P], ident[:])
                elif kind == "oT":
                    wait(pe, o_normed, PAIRS * b + 2 * k + 2)
                    for j in range(2):
                        for t in range(TT):
                            at = (2 * k + j) * P
                            ins = pe.transpose(bank[:, (j * TT + t) * P:(j * TT + t + 1) * P],
                                               o_sb[:, par, t, at:at + P], ident[:])
                elif kind == "sel":
                    pe.matmul(bank[0:2 * RANK, 0:P], ident[:, 1:4 * RANK:2], xn[:, par, 0], start=True, stop=True)
                    ins = pe.matmul(bank[0:2 * RANK, P:2 * P], ident[:, 2:4 * RANK + 1:2], xn[:, par, 0],
                                    start=True, stop=True)
                elif kind == "low":
                    wait(pe, low_made, 2 * b + k + 1)
                    rows = low1[:].rearrange("p a b -> p (a b)") if k == 0 else low2[:].rearrange("p a b c -> p (a b c)")
                    ins = pe.matmul(bank, sel_rows[:, 1, :], rows, start=True, stop=True)
                elif kind == "hid":
                    if k == 0:
                        wait(pe, weff_made, 2 * b + 1)
                    for j in range(2):
                        ins = pe.matmul(bank[:, j * seq:(j + 1) * seq], w1_eff[:, 2 * k + j], xnT[:, par],
                                        start=True, stop=True)
                ins.then_inc(done, 1)

            def scores(st, h):
                b, par, _ = st.batch(0)
                pair, rows = h // 2, slice(DH * (h % 2), DH * (h % 2) + DH)
                if h % 2 == 0:
                    wait(pe, crossed[pair % 2], 32 * (PAIRS // 2 * b + pair // 2 + 1))
                wait(pe, clamp_done, HEADS * b + h + 1 - SCORE_BANKS)
                for t in range(TT):
                    keys = slice(t * P, (t + 1) * P)
                    o = ps_scores[:, h % SCORE_BANKS, t * seq:(t + 1) * seq]
                    pe.matmul(o, heads_T[:, pair, h % 2, 1, keys], heads_T[:, pair, h % 2, 0], start=True, stop=False)
                    ins = pe.matmul(o, heads_T[rows, pair, h % 2, 1, keys], heads_T[rows, pair, 2, 0],
                                    start=False, stop=True)
                ins.then_inc(scores_done, 1)

            def values(st, ahead, h):
                b, par, _ = st.batch(ahead)
                pair = h // 2
                if h == 0:
                    wait(pe, v_split, 4 * b + 4)
                if h in POOL_HEADS:
                    wait(pe, lo_by_pool, len(POOL_HEADS) * b + POOL_HEADS.index(h) + 1)
                else:
                    wait(pe, lo_by_vector, vector_count(b, h))
                if h % 2 == 0:
                    wait(pe, o_normed, PAIRS * b + pair - 1)
                buf = h % RING
                hi = probs[:, buf].bitcast(BF16)[:, 1::2]
                for t in range(TT):
                    at = (t * 2 + h % 2) * (DH + 1)
                    full = ps_o[:, pair % 2, at:at + DH + 1]
                    for u in range(TT):
                        col = slice(u * seq + t * P, u * seq + (t + 1) * P)
                        pe.matmul(full, hi[:, col], v_hi[:, par, u, h], start=(u == 0), stop=False)
                        pe.matmul(full[:, 0:DH], hi[:, col], v_lo[:, par, u, h], start=False, stop=False)
                        ins = pe.matmul(full, probs_lo[:, buf, col], v_hi[:, par, u, h],
                                        start=False, stop=(u == TT - 1))
                ins.then_inc(attended, 1)

            def result(st, first, count):
                b, par, _ = st.batch(-1)
                n = HC + PAIRS
                for j in range(first, first + count):
                    t, i = j // n, j % n
                    tok, pair = slice(t * P, (t + 1) * P), i - HC
                    o = ps_y[:, tok]
                    if j == 0:
                        wait(pe, gelu_done, 4 * b + 4)
                        wait(pe, y_added, b)
                    if t == 0 and pair >= 0 and pair % 2 == 0:
                        wait(pe, oT_copied, 4 * b + pair // 2 + 1)
                    if pair < 0:
                        ins = pe.matmul(o, hid[:, par, i, tok], w2_eff[:, par, i], start=(i == 0), stop=False)
                    else:
                        ins = pe.matmul(o, oT[:, pair, tok], wo_sb[:, pair], start=False, stop=(i == n - 1))
                if first + count == TT * n:
                    ins.then_inc(y_filled, 1)

            def run(st):
                for s in range(HEADS):
                    if "attn" in st.stages:
                        scores(st, s)
                    for task in aux_tasks(st, s, PER_BATCH):
                        aux(st, *task)
                    if "back" in st.stages and s in Y_PRODUCTS:
                        result(st, sum(Y_PRODUCTS.get(i, 0) for i in range(s)), Y_PRODUCTS[s])
                    late = head_of(st, s, VALUES_LAG)
                    if late:
                        values(st, *late)

            run_all(pe, run)

        @block.scalar
        def _(act):
            def run(st):
                for s in range(HEADS):
                    if "attn" in st.stages:
                        b, par, _ = st.batch(0)
                        buf = s % RING
                        wait(act, scores_done, HEADS * b + s + 1)
                        wait(act, probs_done, HEADS * b + s + 1 - RING)
                        nc.scalar.activation(clamped[:, buf], ps_scores[:, s % SCORE_BANKS], ACT.Tanh).then_inc(clamp_done, 1)
                    late = head_of(st, s, 1)
                    if late:
                        ahead, h = late
                        b, par, _ = st.batch(ahead)
                        buf = h % RING
                        wait(act, clamp_done, HEADS * b + h + 1)
                        wait(act, attended, HEADS * b + h + 1 - RING)
                        nc.scalar.activation(probs[:, buf], clamped[:, buf], ACT.Exp, bias=LIFT,
                                             scale=SOFTCLAMP * DH ** -0.5).then_inc(probs_done, 1)
                    for i, kind, k, ahead in aux_tasks(st, s, ("xT", "qk", "v", "oT", "qkT", "hid")):
                        b, par, _ = st.batch(ahead)
                        bank = ps_aux[:, i % AUX_BANKS, :]
                        act.wait_ge(aux_filled[kind], PER_BATCH[kind] * b + k + 1)
                        if kind == "xT":
                            nc.scalar.copy(xnT[:, par], bank[:, seq:2 * seq])
                            nc.scalar.copy(xhT_hi[:, par], bank[:, 0:seq]).then_inc(xT_hi_made, 1)
                        elif kind == "qk":
                            if k == 0:
                                wait(act, aux_filled["qkT"], PAIRS * (b - 1))
                            t, c = k // 4, k % 4
                            nc.scalar.copy(qk[:, par, t, c * 512:(c + 1) * 512], bank).then_inc(qk_copied, 1)
                        elif kind == "v":
                            if k == 0:
                                wait(act, attended, HEADS * (b - 1))
                            t, c = k // 2, k % 2
                            nc.scalar.copy(v_hi[:, par, t, 8 * c:8 * c + 8, 0:DH],
                                           bank.rearrange("p (h d) -> p h d", d=DH)).then_inc(v_hi_made, 1)
                        elif kind == "oT":
                            nc.scalar.copy(oT[:, 2 * k:2 * k + 2], bank.rearrange("p (j t) -> p j t", j=2))\
                                .then_inc(oT_copied, 1)
                        elif kind == "qkT":
                            nc.scalar.copy(heads_T[:, k, 0].rearrange("p j t -> p (j t)"), bank)\
                                .then_inc(qkT_hi_made, 1)
                        elif kind == "hid":
                            for j in range(2):
                                c = 2 * k + j
                                nc.scalar.activation(hid[:, par, c], bank[:, j * seq:(j + 1) * seq], ACT.Gelu,
                                                     bias=b1_col[:, c:c + 1]).then_inc(gelu_done, 1)

            act.wait_ge(setup_made, 8)
            run_all(act, run)

        @block.vector
        def _(dve):
            v = nc.vector
            v.memset(v_hi[:, :, :, :, DH:DH + 1], 1.0)
            dve.wait_ge(consts_loaded, 16 * 11)
            v.tensor_scalar(g_raw, g_raw, 1.0, None, ALU.add).then_inc(setup_made, 1)
            dve.wait_ge(setup_made, 1)
            v.scalar_tensor_tensor(g_bc[:], g_raw[:, 0], DH / SOFTCLAMP, g_raw[:, 1],
                                   ALU.mult, ALU.mult).then_inc(setup_made, 1)
            v.tensor_scalar(w_raw, w_raw, nw_col[:, 0:1], None, ALU.mult).then_inc(setup_made, 1)
            dve.wait_ge(setup_made, 3)
            v.tensor_copy(w_hi[:], w_raw).then_inc(setup_made, 1)
            dve.wait_ge(setup_made, 4)
            v.tensor_tensor(w_lo[:], w_raw, w_hi[:].bitcast(F32), ALU.subtract).then_inc(setup_made, 1)
            dve.wait_ge(setup_turned, 1)
            v.tensor_copy(b1_col[:], ps_aux[:, 2, 0:HC]).then_inc(setup_made, 1)
            v.tensor_copy(w1T[:].rearrange("p a b -> p (a b)"), ps_aux[:, 0]).then_inc(setup_made, 1)
            v.tensor_copy(w2T[:].rearrange("p a b -> p (a b)"), ps_aux[:, 1]).then_inc(setup_made, 1)
            dve.wait_ge(masks_made, 2)
            m1, m2 = mask1[:].rearrange("p a b -> p (a b)"), mask2[:].rearrange("p a b c -> p (a b c)")
            v.tensor_scalar(m1, m1, scale_col[:, 0:1], None, ALU.mult).then_inc(setup_made, 1)
            v.tensor_scalar(m2, m2, scale_col[:, 0:1], None, ALU.mult).then_inc(setup_made, 1)
            dve.wait_ge(setup_made, 10)

            def norm_stats(st):
                b, par, half = st.batch(2)
                dve.wait_ge(x_loaded[par], 16 * (half + 1))
                for t in range(TT):
                    v.bn_stats(stats[:, t], x_in[:, par, t]).then_inc(stats_made, 1)

            def norm_var(st):
                b, par, _ = st.batch(2)
                dve.wait_ge(stats_made, 2 * b + 2)
                v.memset(scratch[:], 0.0)
                for t in range(TT):
                    v.bn_aggr(mean_var[:, t], stats[:, t]).then_inc(meanvar_made, 1)

            def norm_eps(st):
                b, par, _ = st.batch(2)
                dve.wait_ge(meanvar_made, 2 * b + 2)
                v.tensor_scalar(var_eps[:, 0], mean_var[:, :, 1], LN_EPS, None, ALU.add).then_inc(vareps_made, 1)
                v.tensor_scalar(var_eps[:, 1], mean_var[:, :, 1], 1.0 + RMS_EPS, RMS_EPS * LN_EPS,
                                ALU.mult, ALU.add).then_inc(vareps_made, 1)

            def norm_apply(st):
                b, par, _ = st.batch(2)
                dve.wait_ge(rstd_made, b + 1)
                wait(dve, aux_filled["xT"], b)
                wait(dve, aux_filled["sel"], b - 1)
                for j in range(2):
                    for t in range(TT):
                        o = xn[:, par, t] if j == 0 else xh[:, t]
                        ins = v.tensor_scalar(o, x_in[:, par, t], mean_var[:, t, 0:1], rstd[:, j, t:t + 1],
                                              ALU.subtract, ALU.mult)
                ins.then_inc(xn_made, 1)

            def xT_lo(st, bank):
                b, par, _ = st.batch(2)
                dve.wait_ge(xT_hi_made, b + 1)
                v.tensor_tensor(xhT_lo[:, par], bank[:, 0:seq], xhT_hi[:, par].bitcast(F32), ALU.subtract).then_inc(xT_split, 1)

            def sum_squares(st, k):
                b, _, _ = st.batch(1)
                dve.wait_ge(sq_made, 8 * b + k + 1)
                v.tensor_reduce(norm2[:, 8 * k:8 * k + 8], sq[:, k % 2].rearrange("p (h d) -> p h d", d=DH),
                                AX_X, ALU.add).then_inc(norm2_made, 1)

            def rsqrt_safe(st):
                b, _, _ = st.batch(1)
                dve.wait_ge(norm2_made, 8 * b + 8)
                v.tensor_scalar(norm2_safe[:], norm2[:], NORM2_MIN, None, ALU.max).then_inc(seed_made, 1)

            def rsqrt_seed(st):
                b, _, _ = st.batch(1)
                dve.wait_ge(seed_made, 3 * b + 1)
                wait(dve, qk_normed, 4 * b)
                v.tensor_scalar(minus_half_norm2[:], norm2_safe[:], -0.5, None, ALU.mult).then_inc(seed_made, 1)
                v.tensor_scalar(rnorm[:].bitcast(I32), norm2_safe[:].bitcast(I32), -0.5, RSQRT_SEED,
                                ALU.mult, ALU.add).then_inc(seed_made, 1)

            def normalise(st, c):
                b, par, _ = st.batch(1)
                if c == 0:
                    dve.wait_ge(newton_step, 12 * b + 12)
                if c % 2 == 0:
                    dve.wait_ge(q_scaled, 4 * b + c + 2)
                part = qk[:, par].rearrange("p t (j n) -> p (t j) n", j=2)[:, :, c * 4 * DH:(c + 1) * 4 * DH]\
                    .rearrange("p a (h d) -> p a h d", d=DH)
                r = rnorm[:].rearrange("p (a h) -> p a h", h=HEADS)[:, :, 4 * c:4 * c + 4]
                v.tensor_tensor(part, part, r.unsqueeze(3).to_broadcast([P, 2 * TT, 4, DH]), ALU.mult)\
                    .then_inc(qk_normed, 1)

            def lo_part(st, ahead, h):
                b, _, _ = st.batch(ahead)
                buf = h % RING
                dve.wait_ge(probs_done, HEADS * b + h + 1)
                v.tensor_tensor(probs_lo[:, buf], probs[:, buf], probs[:, buf].bitcast(BF16)[:, 1::2], ALU.subtract)\
                    .then_inc(lo_by_vector, 1)

            def divide(st, ahead, pair):
                b, par, _ = st.batch(ahead)
                got = ps_o[:, pair % 2, 0:4 * (DH + 1)].rearrange("p (a d) -> p a d", d=DH + 1)
                dve.wait_ge(attended, HEADS * b + 2 * pair + 2)
                v.reciprocal(rden[:, pair % 2], got[:, :, DH]).then_inc(rden_made, 1)
                dve.wait_ge(rden_made, PAIRS * b + pair + 1)
                if pair == 0:
                    wait(dve, aux_filled["oT"], 4 * (b - 1))
                v.tensor_tensor(o_sb[:, par, :, pair * P:(pair + 1) * P].rearrange("p t (j d) -> p t j d", d=DH),
                                got[:, :, 0:DH].rearrange("p (t j) d -> p t j d", j=2),
                                rden[:, pair % 2].rearrange("p (t j) -> p t j", j=2).unsqueeze(3)
                                .to_broadcast([P, TT, 2, DH]), ALU.mult).then_inc(o_normed, 1)

            def result(st):
                b, par, half = st.batch(-2)
                dve.wait_ge(y_filled, b + 1)
                dve.wait_ge(xb2_made, b + 1)
                wait(dve, y_stored[par], 16 * half)
                v.tensor_tensor(y_sb[:, par].rearrange("p t d -> p (t d)"), ps_y[:, 0:seq],
                                x_b2[:].rearrange("p t d -> p (t d)"), ALU.add).then_inc(y_added, 1)

            def aux(st, i, kind, k, ahead):
                b, par, _ = st.batch(ahead)
                bank = ps_aux[:, i % AUX_BANKS, :]
                if kind == "xT":
                    xT_lo(st, bank)
                elif kind == "v":
                    dve.wait_ge(v_hi_made, 4 * b + k + 1)
                    t, c = k // 2, k % 2
                    v.tensor_tensor(v_lo[:, par, t, 8 * c:8 * c + 8], bank.rearrange("p (h d) -> p h d", d=DH),
                                    v_hi[:, par, t, 8 * c:8 * c + 8, 0:DH], ALU.subtract).then_inc(v_split, 1)
                elif kind == "qkT":
                    dve.wait_ge(qkT_hi_made, PAIRS * b + k + 1)
                    v.tensor_tensor(heads_T[:, k, 2].rearrange("p j t -> p (j t)"), bank,
                                    heads_T[:, k, 0].rearrange("p j t -> p (j t)"), ALU.subtract)\
                        .then_inc(qkT_split, 1)
                elif kind == "sel":
                    dve.wait_ge(aux_filled["sel"], b + 1)
                    wait(dve, aux_filled["low"], 2 * b)
                    v.tensor_copy(sel_rows[:].rearrange("p a b -> p (a b)"), bank[0:2 * RANK, 0:2 * P])\
                        .then_inc(sel_copied, 1)
                    dve.wait_ge(sel_copied, b + 1)
                    even = sel_rows[:, 0]
                    v.tensor_tensor(low1[:], even.unsqueeze(1).to_broadcast([2 * RANK, RANK, P]), mask1[:], ALU.mult)\
                        .then_inc(low_made, 1)
                    v.tensor_tensor(low2[:], even.rearrange("p (o t) -> p t o", t=HC).unsqueeze(2)
                                    .to_broadcast([2 * RANK, HC, RANK, P // RANK]), mask2[:], ALU.mult)\
                        .then_inc(low_made, 1)
                elif kind == "low":
                    dve.wait_ge(aux_filled["low"], 2 * b + k + 1)
                    if k == 1:
                        wait(dve, y_filled, b - 1)
                    o, base = (w1_eff[:], w1T) if k == 0 else (w2_eff[:, par], w2T)
                    v.tensor_tensor(o, bank.rearrange("p (c n) -> p c n", c=HC), base[:], ALU.add)\
                        .then_inc(weff_made, 1)

            def run(st):
                for s in range(HEADS):
                    if "store" in st.stages and s == 0:
                        result(st)
                    if "norm" in st.stages and s == 10:
                        norm_apply(st)
                    if "front" in st.stages and s in NORMALISE[:2]:
                        normalise(st, NORMALISE.index(s))
                    tasks = list(aux_tasks(st, s, ("xT", "v", "qkT", "sel", "low")))
                    if s == 0:
                        for task in tasks:
                            aux(st, *task)
                    late = head_of(st, s, 1)
                    if late and late[1] not in POOL_HEADS:
                        lo_part(st, *late)
                    late = head_of(st, s, VALUES_LAG + 1)
                    if late and late[1] % 2 == 1:
                        divide(st, late[0], late[1] // 2)
                    if s > 0:
                        for task in tasks:
                            aux(st, *task)
                    if "front" in st.stages:
                        if s in NORMALISE[2:]:
                            normalise(st, NORMALISE.index(s))
                        for k in SUMS.get(s, ()):
                            sum_squares(st, k)
                        if s == 7:
                            rsqrt_safe(st)
                            rsqrt_seed(st)
                    if "norm" in st.stages:
                        if s == 3:
                            norm_stats(st)
                            norm_var(st)
                            norm_eps(st)

            run_all(dve, run)

        @block.gpsimd
        def _(pool):
            g = nc.gpsimd
            g.memset(minus_half[:], -0.5)
            g.memset(newton_c[:], 1.5)
            g.memset(mask1[:], 0.0)
            g.memset(mask2[:], 0.0)
            g.memset(ident[:], 0.0).then_inc(ident_made, 1)
            pool.wait_ge(ident_made, 1)
            g.affine_select(out=ident[:], in_=ident[:], compare_op=ALU.not_equal, fill=1.0, base=0,
                            pattern=[[-1, P]], channel_multiplier=1).then_inc(ident_made, 1)
            g.affine_select(out=mask1[:], in_=mask1[:], compare_op=ALU.not_equal, fill=1.0, base=0,
                            pattern=[[-1, RANK], [0, P]], channel_multiplier=1).then_inc(masks_made, 1)
            g.affine_select(out=mask2[:], in_=mask2[:], compare_op=ALU.not_equal, fill=1.0, base=-RANK,
                            pattern=[[0, HC], [-1, RANK], [0, P // RANK]], channel_multiplier=1)\
                .then_inc(masks_made, 1)

            def square(st, k):
                b, par, _ = st.batch(1)
                t, c = k // 4, k % 4
                part = qk[:, par, t, c * 512:(c + 1) * 512]
                pool.wait_ge(qk_copied, 8 * b + k + 1)
                wait(pool, norm2_made, 8 * b + k - 1)
                g.tensor_tensor(sq[:, k % 2], part, part, ALU.mult).then_inc(sq_made, 1)

            def scale_queries(st, k):
                b, par, _ = st.batch(1)
                t, c = k // 4, k % 4
                part = qk[:, par, t, c * 512:(c + 1) * 512]
                pool.wait_ge(sq_made, 8 * b + k + 1)
                g.tensor_tensor(part, part, g_bc[:, c * 512:(c + 1) * 512], ALU.mult).then_inc(q_scaled, 1)

            def newton(st, turn):
                b, _, _ = st.batch(1)
                if turn == 0:
                    pool.wait_ge(seed_made, 3 * b + 3)
                n = 12 * b + 4 * turn

                def after(k):
                    wait(pool, newton_step, n + k)

                after(0)
                g.tensor_tensor(newton_a[:], rnorm[:], rnorm[:], ALU.mult).then_inc(newton_step, 1)
                after(1)
                g.tensor_tensor(newton_b[:], newton_a[:], minus_half_norm2[:], ALU.mult).then_inc(newton_step, 1)
                after(2)
                g.tensor_tensor(newton_a[:], newton_b[:], newton_c[:], ALU.add).then_inc(newton_step, 1)
                after(3)
                g.tensor_tensor(rnorm[:], rnorm[:], newton_a[:], ALU.mult).then_inc(newton_step, 1)

            def run(st):
                for s in range(HEADS):
                    late = head_of(st, s, 1)
                    if late and late[1] in POOL_HEADS:
                        ahead, h = late
                        b, _, _ = st.batch(ahead)
                        buf = h % RING
                        pool.wait_ge(probs_done, HEADS * b + h + 1)
                        g.tensor_tensor(probs_lo[:, buf], probs[:, buf], probs[:, buf].bitcast(BF16)[:, 1::2],
                                        ALU.subtract).then_inc(lo_by_pool, 1)
                    if "front" in st.stages:
                        for k in SQUARES.get(s, ()):
                            square(st, k)
                        for k in SCALES.get(s, ()):
                            scale_queries(st, k)
                        for turn in NEWTON.get(s, ()):
                            newton(st, turn)
                    if "back" in st.stages and s == 9:
                        b, par, half = st.batch(-1)
                        pool.wait_ge(res_loaded[par], 16 * (half + 1))
                        wait(pool, y_added, b)
                        g.tensor_tensor(x_b2[:], x_res[:, par], b2_bc[:].unsqueeze(1).to_broadcast([P, TT, P]),
                                        ALU.add).then_inc(xb2_made, 1)
                    if "norm" in st.stages and s == 6:
                        b, _, _ = st.batch(2)
                        pool.wait_ge(vareps_made, 2 * b + 2)
                        wait(pool, xn_made, b)
                        g.tensor_tensor(rstd[:].rearrange("p a b -> p (a b)"),
                                        var_eps[:].rearrange("p a b -> p (a b)"), minus_half[:], ALU.pow)\
                            .then_inc(rstd_made, 1)

            pool.wait_ge(consts_loaded, 16 * 11)
            pool.wait_ge(setup_made, 2)
            run_all(pool, run)


_INS = ["L0_attn_tokens", "L0_attn_norm_w", "L0_attn_Wq", "L0_attn_Wkv", "L0_attn_Wo", "L0_attn_q_gamma",
        "L0_attn_k_gamma", "L0_ffn_W1", "L0_ffn_b1", "L0_ffn_W2", "L0_ffn_b2", "L0_ffn_scale"]


def kernel(**inputs):
    import numpy as _np
    import concourse.bacc as _bacc
    from concourse import mybir as _mybir
    from concourse.bass_utils import run_bass_kernel_spmd as _run

    nc = _bacc.Bacc("TRN2", target_bir_lowering=False, num_devices=1)
    arrays, args = {}, []
    for name in _INS:
        a = _np.ascontiguousarray(inputs[name])
        if a.ndim == 0:
            a = a.reshape(1)
        arrays[f"in_{name}_dram"] = a
        args.append(nc.dram_tensor(f"in_{name}_dram", a.shape, _mybir.dt.from_np(a.dtype), kind="ExternalInput").ap())
    shape = tuple(inputs["L0_attn_tokens"].shape)
    out = nc.dram_tensor("out_0_dram", shape, _mybir.dt.float32, kind="ExternalOutput").ap()
    block_kernel(nc, *args, out)
    r = _run(nc, [arrays], core_ids=[0])
    return r.results[0]["out_0_dram"]
```

```python
from contextlib import ExitStack

import concourse.bass as bass
from concourse import mybir

F32 = mybir.dt.float32
F32R = mybir.dt.float32r
BF16 = mybir.dt.bfloat16
F16 = mybir.dt.float16
I32 = mybir.dt.int32
ALU = mybir.AluOpType
ACT = mybir.ActivationFunctionType
AX_X = mybir.AxisListType.X

P = 128
HEADS = 16
DH = 64
PAIRS = HEADS // 2
HIDDEN = 512
HC = HIDDEN // P
RANK = 4
BLOCK = 32
ROWS = 2 * BLOCK + 2 * RANK
SOFTCLAMP = 50.0
LN_EPS = 1e-5
RMS_EPS = 2.0 ** -23
NORM2_MIN = 1e-24
RSQRT_SEED = float(0x5F3759DF)
LIFT = 4.1588830833596715

AUX_BANKS = 3
AUX = [
    (1, "qk", 2, 1), (1, "qk", 3, 1), (1, "qk", 4, 1),
    (2, "qkT", 4, 0), (2, "qkT", 5, 0),
    (3, "qk", 5, 1),
    (4, "oT", 0, -1), (4, "oT", 1, -1), (4, "qk", 6, 1),
    (5, "qk", 7, 1), (5, "low", 0, 0), (5, "v", 0, 1),
    (6, "oT", 2, -1), (6, "v", 1, 1),
    (7, "oT", 3, -1), (7, "qkT", 6, 0),
    (8, "qkT", 7, 0), (8, "v", 2, 1),
    (9, "hid", 0, 0), (9, "hid", 1, 0),
    (10, "low", 1, 0), (10, "v", 3, 1),
    (11, "xhT", 0, 2),
    (12, "qkT", 0, 1), (12, "qkT", 1, 1),
    (13, "xnT", 0, 2),
    (14, "qk", 0, 2), (14, "qkT", 2, 1),
    (15, "qkT", 3, 1), (15, "qk", 1, 2),
]
assert len(AUX) % AUX_BANKS == 0
PER_BATCH = {"xhT": 1, "xnT": 1, "qk": 8, "v": 4, "oT": 4, "low": 2, "qkT": 8, "hid": 2}
STAGE = {2: "turn", 1: "front", 0: "attn", -1: "back"}
SCORE_BANKS = 2
RING = 4
VALUES_LAG = 3
POOL_HEADS = (0, 5, 9, 10, 11, 12, 13, 14)
VECTOR_STEPS = [
    [("result",), ("lo",), ("sum", 0)],
    [("norm_stats",), ("sum", 1), ("divide",)],
    [("lo",), ("splits",), ("sum", 2)],
    [("divide",), ("lo",)],
    [("lo",), ("sum", 3)],
    [("divide",), ("updates",), ("sum", 4), ("splits",), ("sum", 5), ("lo",)],
    [("sum", 6), ("splits",), ("sum", 7)],
    [("seed",), ("divide",), ("splits",), ("lo",)],
    [("splits",), ("lo",)],
    [("lo",), ("divide",), ("norm_apply",), ("normalise", 0)],
    [("normalise", 1), ("updates",), ("splits",), ("normalise", 2)],
    [("splits",), ("divide",)],
    [("splits",)],
    [("select",), ("divide",)],
    [("normalise", 3), ("splits",)],
    [("splits",), ("divide",)],
]
POOL_STEPS = [
    [("square", 0), ("square", 1)],
    [("lo",), ("rstd",)],
    [],
    [("square", 2), ("square", 3), ("square", 4), ("scale", 0)],
    [("square", 5), ("bias",)],
    [("square", 6), ("square", 7)],
    [("lo",)],
    [("scale", 4), ("newton", 0), ("newton", 1), ("newton", 2)],
    [("scale", 1)],
    [("scale", 5)],
    [("lo",)],
    [("lo",)],
    [("lo",)],
    [("lo",)],
    [("lo",)],
    [("lo",)],
]
SELECT_SLOT = 3
STORE_SLOT = 12
Y_PRODUCTS = {3: 2, 5: 1, 6: 1, 7: 2, 8: 1, 9: 5, 10: 5, 11: 1, 12: 3, 13: 1, 14: 1, 15: 1}


class Step:

    def __init__(self, half, odd, stages):
        self.half, self.odd, self.stages = half, odd, stages
        self.number = None if not isinstance(half, int) else 2 * half + odd

    def batch(self, ahead):
        m = self.odd + ahead
        return 2 * self.half + m, m % 2, self.half + m // 2


def stages_of(n, batches):
    out = set()
    if 0 <= n < batches:
        out.add("attn")
    if 0 <= n + 1 < batches:
        out.add("front")
    if 0 <= n + 2 < batches:
        out.add("turn")
        if n > -2:
            out.add("norm")
    if 0 <= n + 3 < batches:
        out.add("load")
    if 0 <= n - 1 < batches:
        out.add("back")
    if 0 <= n - 2 < batches:
        out.add("store")
    return out


def block_kernel(nc, tokens, norm_w, wq, wkv, wo, q_gamma, k_gamma, w1, b1, w2, b2, scale, out):
    batches, seq, dim = tokens.shape
    TT = seq // P
    assert dim == P and TT == 2 and wq.shape[1] == HEADS * DH and w1.shape[0] == HIDDEN and batches % 2 == 0
    QK = 2 * HEADS * DH
    QKV = QK + HEADS * DH

    with ExitStack() as ctx:
        def sb(name, shape, dt=F32):
            return ctx.enter_context(nc.sbuf_tensor(name, shape, dt))

        def sem(name):
            return ctx.enter_context(nc.semaphore(name))

        ps_scores = ctx.enter_context(nc.psum_tensor("ps_scores", [P, SCORE_BANKS, 512], F32))
        ps_o = ctx.enter_context(nc.psum_tensor("ps_o", [P, 2, 512], F32))
        ps_aux = ctx.enter_context(nc.psum_tensor("ps_aux", [P, AUX_BANKS, 512], F32))
        ps_y = ctx.enter_context(nc.psum_tensor("ps_y", [P, 512], F32))

        ident = sb("ident", [P, P])
        w_hi = sb("w_hi", [P, QKV], F32R)
        w_lo = sb("w_lo", [P, QKV], F32R)
        wo_sb = sb("wo_sb", [P, PAIRS, P])
        w1T = sb("w1T", [P, HC, P])
        w2T = sb("w2T", [P, HC, P])
        nw_col = sb("nw_col", [P, 1])
        g_bc = sb("g_bc", [P, HEADS * DH])
        b1_raw = sb("b1_raw", [HC, P])
        b1_col = sb("b1_col", [P, HC])
        b2_bc = sb("b2_bc", [P, P])
        scale_col = sb("scale_col", [P, 1])
        mask1 = sb("mask1", [ROWS, RANK, P], F16)
        mask2 = sb("mask2", [ROWS, HC, RANK, P // RANK], F16)
        minus_half = sb("minus_half", [P, 4])
        scratch = sb("scratch", [P, 1])
        newton_c = sb("newton_c", [P, TT * 2 * HEADS])

        x_in = sb("x_in", [P, 2, TT, P])
        x_res = sb("x_res", [P, 2, TT, P])
        x_b2 = sb("x_b2", [P, TT, P])
        stats = sb("stats", [P, TT, 6])
        mean_var = sb("mean_var", [P, TT, 2])
        var_eps = sb("var_eps", [P, 2, TT])
        rstd = sb("rstd", [P, 2, TT])
        xn = sb("xn", [P, 2, TT, P])
        xh = sb("xh", [P, TT, P])
        xnT = sb("xnT", [P, 2, seq])
        xhT_hi = sb("xhT_hi", [P, 2, seq], F32R)
        xhT_lo = sb("xhT_lo", [P, 2, seq], F32R)
        qk = sb("qk", [P, 2, TT, QK])
        early = qk[:, 1].rearrange("p t n -> p (t n)")
        w_raw = early[:, 0:QKV]
        w1_raw = early[:, QKV:QKV + HIDDEN].rearrange("p (c n) -> p c n", c=HC)
        w2_raw = early[:, QKV + HIDDEN:QKV + 2 * HIDDEN]
        sq = sb("sq", [P, 2, 512])
        norm2 = sb("norm2", [P, TT * 2 * HEADS])
        norm2_safe = sb("norm2_safe", [P, TT * 2 * HEADS])
        minus_half_norm2 = sb("minus_half_norm2", [P, TT * 2 * HEADS])
        rnorm = sb("rnorm", [P, TT * 2 * HEADS])
        newton_a = sb("newton_a", [P, TT * 2 * HEADS])
        newton_b = sb("newton_b", [P, TT * 2 * HEADS])
        heads_T = sb("heads_T", [P, PAIRS, 3, 2, seq], F16)
        v_hi = sb("v_hi", [P, 2, TT, HEADS, DH + 1], BF16)
        v_lo = sb("v_lo", [P, 2, TT, HEADS, DH], BF16)
        clamped = sb("clamped", [P, RING, TT * seq])
        probs = sb("probs", [P, RING, TT * seq])
        probs_lo = sb("probs_lo", [P, RING, TT * seq], F16)
        rden = sb("rden", [P, 2, 4])
        o_sb = sb("o_sb", [P, 2, TT, HEADS * DH])
        oT = sb("oT", [P, PAIRS, seq])
        sel_raw = sb("sel_raw", [ROWS, 2, P])
        sel_rows = sb("sel_rows", [ROWS, 2, P], F16)
        low1 = sb("low1", [ROWS, RANK, P], F16)
        low2 = sb("low2", [ROWS, HC, RANK, P // RANK], F16)
        w1_eff = sb("w1_eff", [P, HC, P])
        w2_eff = sb("w2_eff", [P, 2, HC, P])
        hid = sb("hid", [P, 2, HC, seq])
        g_raw = hid[:].rearrange("p a c t -> p a (c t)")
        y_sb = sb("y_sb", [P, 2, TT, P])

        w_loaded = [sem(f"w_loaded{i}") for i in range(3)]
        ffn_loaded = sem("ffn_loaded")
        gammas_loaded = sem("gammas_loaded")
        consts_loaded = sem("consts_loaded")
        minus_half_made = sem("minus_half_made")
        ident_made = sem("ident_made")
        masks_made = sem("masks_made")
        rows_cleared = sem("rows_cleared")
        rows_loaded = sem("rows_loaded")
        w_scaled = sem("w_scaled")
        w_hi_made = sem("w_hi_made")
        w_split = sem("w_split")
        ffn_turned = sem("ffn_turned")
        ffn_copied = sem("ffn_copied")
        gammas_made = sem("gammas_made")
        x_loaded = [sem(f"x_loaded{i}") for i in range(2)]
        res_loaded = [sem(f"res_loaded{i}") for i in range(2)]
        y_stored = [sem(f"y_stored{i}") for i in range(2)]
        stats_made = sem("stats_made")
        meanvar_made = sem("meanvar_made")
        vareps_made = sem("vareps_made")
        rstd_made = sem("rstd_made")
        xn_made = sem("xn_made")
        sq_made = sem("sq_made")
        norm2_made = sem("norm2_made")
        seed_made = sem("seed_made")
        newton_step = sem("newton_step")
        q_scaled = sem("q_scaled")
        qk_normed = sem("qk_normed")
        scores_done = sem("scores_done")
        clamp_done = sem("clamp_done")
        probs_done = sem("probs_done")
        lo_by_vector = sem("lo_by_vector")
        lo_by_pool = sem("lo_by_pool")
        attended = sem("attended")
        rden_made = sem("rden_made")
        o_normed = sem("o_normed")
        aux_filled = {k: sem(f"{k}_filled") for k in PER_BATCH}
        xT_hi_made = sem("xT_hi_made")
        xT_split = sem("xT_split")
        xnT_copied = sem("xnT_copied")
        qk_copied = sem("qk_copied")
        v_hi_made = sem("v_hi_made")
        v_split = sem("v_split")
        qkT_hi_made = sem("qkT_hi_made")
        qkT_split = sem("qkT_split")
        second_moved = [sem(f"second_moved{i}") for i in range(2)]
        crossed = [sem(f"crossed{i}") for i in range(2)]
        oT_copied = sem("oT_copied")
        sel_copied = sem("sel_copied")
        low_made = sem("low_made")
        weff_made = sem("weff_made")
        gelu_done = sem("gelu_done")
        y_filled = sem("y_filled")
        xb2_made = sem("xb2_made")
        y_added = sem("y_added")

        AUX_READ = {"xhT": (xT_split, 1), "xnT": (xnT_copied, 1), "qk": (qk_copied, 1),
                    "v": (v_split, 1), "qkT": (qkT_split, 1),
                    "oT": (oT_copied, 1), "low": (weff_made, 1), "hid": (gelu_done, 2)}

        def wait(eng, s, value):
            if isinstance(value, int) and value <= 0:
                return
            eng.wait_ge(s, value)

        def wait_bank(eng, st, index):
            for back in range(1, 3 * len(AUX)):
                i = index - back * AUX_BANKS
                rounds, j = i // len(AUX), i % len(AUX)
                if rounds < -1:
                    return
                _, kind, k, ahead = AUX[j]
                if STAGE[ahead] in (st.stages if rounds == 0 else st.before):
                    s, per = AUX_READ[kind]
                    wait(eng, s, per * PER_BATCH[kind] * st.batch(ahead + rounds)[0] + per * (k + 1))
                    return

        def aux_tasks(st, slot, kinds):
            for i, (s, kind, k, ahead) in enumerate(AUX):
                if s == slot and kind in kinds and STAGE[ahead] in st.stages:
                    yield i, kind, k, ahead

        def head_of(st, slot, lag):
            ahead, head = (0, slot - lag) if slot >= lag else (-1, slot - lag + HEADS)
            there = "attn" if ahead == 0 else "back"
            return (ahead, head) if there in st.stages else None

        def plan(run):
            def straight(n):
                st = Step(n // 2, n % 2, stages_of(n, batches))
                st.before = stages_of(n - 1, batches)
                run(st)

            first, last = 3, batches - 4
            for n in range(-2, first):
                straight(n)
            yield first // 2, (last + 1) // 2
            for n in range(last + 1, batches + 2):
                straight(n)

        def run_all(eng, run):
            for start, end in plan(run):
                with eng.Fori(start, end) as i:
                    for odd in (1, 2):
                        st = Step(i, odd, stages_of(3, batches))
                        st.before = st.stages
                        run(st)

        def vector_count(b, h):
            return (HEADS - len(POOL_HEADS)) * b + len([i for i in range(h + 1) if i not in POOL_HEADS])

        block = ctx.enter_context(nc.Block())

        @block.sync
        def _(sp):
            def x_of(b):
                return tokens[bass.ds(b, 1)].rearrange("o (t p) d -> p (o t) d", p=P)

            sp.dma_start(x_in[:, 0], tokens[0].rearrange("(t p) d -> p t d", p=P)).then_inc(x_loaded[0], 16)
            sp.dma_start(nw_col[:], norm_w.rearrange("(p o) -> p o", o=1)).then_inc(w_loaded[0], 16)
            sp.dma_start(w_raw[:, 0:HEADS * DH], wq).then_inc(w_loaded[0], 16)
            sp.dma_start(w_raw[:, HEADS * DH:QK], wkv[:, 0:HEADS * DH]).then_inc(w_loaded[1], 16)
            sp.dma_start(w_raw[:, QK:QKV], wkv[:, HEADS * DH:2 * HEADS * DH]).then_inc(w_loaded[2], 16)
            sp.dma_start(w1_raw, w1.rearrange("(c p) d -> p c d", p=P)).then_inc(ffn_loaded, 16)
            sp.dma_start(w2_raw, w2).then_inc(ffn_loaded, 16)
            sp.dma_start(x_in[:, 1], tokens[1].rearrange("(t p) d -> p t d", p=P)).then_inc(x_loaded[1], 16)
            sp.dma_start(b1_raw[:], b1.rearrange("(c p) -> c p", p=P)).then_inc(ffn_loaded, 16)
            for j, gamma in enumerate((q_gamma, k_gamma)):
                sp.dma_start(g_raw[:, j], gamma.rearrange("(o h) d -> o (h d)", o=1).to_broadcast([P, HEADS * DH]))\
                    .then_inc(gammas_loaded, 16)
            sp.dma_start(b2_bc[:], b2.rearrange("(o d) -> o d", o=1).to_broadcast([P, P])).then_inc(consts_loaded, 16)
            sp.dma_start(scale_col[:], scale.rearrange("(o d) -> o d", o=1).to_broadcast([P, 1])).then_inc(consts_loaded, 16)
            sp.dma_start(wo_sb[:], wo.rearrange("(q p) n -> p q n", p=P)).then_inc(consts_loaded, 16)

            def load_rows(st):
                b, par, _ = st.batch(1)
                normed, used = [v if isinstance(v, int) else sp.to_reg(v) for v in (b + 1, 3 * b)]
                sp.wait_ge(xn_made, normed)
                if isinstance(b, int) and b == 0:
                    sp.wait_ge(rows_cleared, 1)
                wait(sp, sel_copied, used)
                for j in range(2):
                    for at in range(0, ROWS, BLOCK):
                        sp.dma_start(sel_raw[at:at + 2 * RANK, j], xn[1 + j:4 * RANK + j:2, par, 0])\
                            .then_inc(rows_loaded, 16)

            def move_second(st, k, ahead):
                b, _, _ = st.batch(ahead)
                pair = heads_T[:, k].rearrange("p a j t -> p (a j) t")
                sp.wait_ge(qkT_hi_made, PAIRS * b + k + 1)
                sp.dma_start(pair[DH:P, 2:4], pair[DH:P, 0:2]).then_inc(second_moved[k % 2], 16)

            def cross(st, k, ahead):
                b, _, _ = st.batch(ahead)
                pair = heads_T[:, k].rearrange("p a j t -> p (a j) t")
                split, moved, before = [v if isinstance(v, int) else sp.to_reg(v) for v in (
                    PAIRS * b + k + 1, 16 * (PAIRS // 2 * b + k // 2 + 1), 32 * (PAIRS // 2 * b + k // 2))]
                sp.wait_ge(qkT_split, split)
                sp.wait_ge(second_moved[k % 2], moved)
                wait(sp, crossed[k % 2], before)
                sp.dma_start(pair[DH:P, 0:2], pair[0:DH, 0:6:5]).then_inc(crossed[k % 2], 16)
                sp.dma_start(pair[0:DH, 2:4], pair[DH:P, 2:6:3]).then_inc(crossed[k % 2], 16)

            def run(st):
                if "load" in st.stages:
                    b, par, _ = st.batch(3)
                    if not (isinstance(b, int) and b < 2):
                        wait(sp, xn_made, b - 1)
                        sp.dma_start(x_in[:, par], x_of(b)).then_inc(x_loaded[par], 16)
                if "attn" in st.stages:
                    b, par, _ = st.batch(0)
                    wait(sp, xb2_made, b - 1)
                    sp.dma_start(x_res[:, par], x_of(b)).then_inc(res_loaded[par], 16)
                for s in range(HEADS):
                    if "front" in st.stages and s == SELECT_SLOT:
                        load_rows(st)
                    for _, _, k, ahead in aux_tasks(st, s, ("qkT",)):
                        move_second(st, k, ahead)
                    for slot, kind, k, ahead in AUX:
                        if kind == "qkT" and slot == (s - 1) % HEADS and STAGE[ahead] in (st.stages if s else st.before):
                            cross(st, k, ahead if s else ahead - 1)
                    if "store" in st.stages and s == STORE_SLOT:
                        b, par, _ = st.batch(-2)
                        wait(sp, y_added, b + 1)
                        sp.dma_start(out[bass.ds(b, 1)].rearrange("o (t p) d -> p (o t) d", p=P),
                                     y_sb[:, par]).then_inc(y_stored[par], 16)

            run_all(sp, run)
            for par in range(2):
                sp.wait_ge(y_stored[par], 16 * (batches // 2))

        @block.tensor
        def _(pe):
            def mm3(o, hi_l, lo_l, hi_r, lo_r, last=True):
                pe.matmul(o, hi_l, hi_r, start=True, stop=False)
                pe.matmul(o, hi_l, lo_r, start=False, stop=False)
                return pe.matmul(o, lo_l, hi_r, start=False, stop=last)

            pe.wait_ge(ffn_loaded, 16 * 3)
            pe.wait_ge(ident_made, 2)
            for c in range(HC):
                pe.transpose(ps_scores[:, 0, c * P:(c + 1) * P], w1_raw[:, c], ident[:])
            for c in range(HC):
                pe.transpose(ps_scores[:, 1, c * P:(c + 1) * P], w2_raw[:, c * P:(c + 1) * P], ident[:])
            pe.transpose(ps_o[:, 0, 0:HC], b1_raw[:], ident[0:HC, 0:HC]).then_inc(ffn_turned, 1)

            def aux(st, i, kind, k, ahead):
                wait_bank(pe, st, i)
                bank = ps_aux[:, i % AUX_BANKS, :]
                b, par, _ = st.batch(ahead)
                done = aux_filled[kind]
                if kind in ("xhT", "xnT"):
                    wait(pe, xn_made, b + 1)
                    for t in range(TT):
                        ins = pe.transpose(bank[:, t * P:(t + 1) * P], xh[:, t] if kind == "xhT" else xn[:, par, t],
                                           ident[:])
                elif kind == "qk":
                    t, c = k // 4, k % 4
                    if k == 0:
                        if isinstance(b, int) and b == 0:
                            pe.wait_ge(w_split, 3)
                        wait(pe, xT_split, b + 1)
                    tok, col = slice(t * P, (t + 1) * P), slice(c * 512, (c + 1) * 512)
                    ins = mm3(bank, xhT_hi[:, par, tok], xhT_lo[:, par, tok], w_hi[:, col], w_lo[:, col])
                elif kind == "v":
                    t, c = k // 2, k % 2
                    tok, col = slice(t * P, (t + 1) * P), slice(QK + c * 512, QK + (c + 1) * 512)
                    ins = mm3(bank, xhT_hi[:, par, tok], xhT_lo[:, par, tok], w_hi[:, col], w_lo[:, col])
                elif kind == "qkT":
                    if k % 2 == 0:
                        wait(pe, qk_normed, 4 * b + k // 2 + 1)
                    for j in range(2):
                        for t in range(TT):
                            at = j * HEADS * DH + k * P
                            ins = pe.transpose(bank[:, (j * TT + t) * P:(j * TT + t + 1) * P],
                                               qk[:, par, t, at:at + P], ident[:])
                elif kind == "oT":
                    wait(pe, o_normed, PAIRS * b + 2 * k + 2)
                    for j in range(2):
                        for t in range(TT):
                            at = (2 * k + j) * P
                            ins = pe.transpose(bank[:, (j * TT + t) * P:(j * TT + t + 1) * P],
                                               o_sb[:, par, t, at:at + P], ident[:])
                elif kind == "low":
                    wait(pe, low_made, 2 * b + k + 1)
                    rows = low1[:].rearrange("p a b -> p (a b)") if k == 0 else low2[:].rearrange("p a b c -> p (a b c)")
                    ins = pe.matmul(bank, sel_rows[:, 1, :], rows, start=True, stop=True)
                elif kind == "hid":
                    if k == 0:
                        wait(pe, weff_made, 2 * b + 1)
                    for j in range(2):
                        ins = pe.matmul(bank[:, j * seq:(j + 1) * seq], w1_eff[:, 2 * k + j], xnT[:, par],
                                        start=True, stop=True)
                ins.then_inc(done, 1)

            def scores(st, h):
                b, par, _ = st.batch(0)
                pair, rows = h // 2, slice(DH * (h % 2), DH * (h % 2) + DH)
                if h % 2 == 0:
                    wait(pe, crossed[pair % 2], 32 * (PAIRS // 2 * b + pair // 2 + 1))
                wait(pe, clamp_done, HEADS * b + h + 1 - SCORE_BANKS)
                for t in range(TT):
                    keys = slice(t * P, (t + 1) * P)
                    o = ps_scores[:, h % SCORE_BANKS, t * seq:(t + 1) * seq]
                    pe.matmul(o, heads_T[:, pair, h % 2, 1, keys], heads_T[:, pair, h % 2, 0], start=True, stop=False)
                    ins = pe.matmul(o, heads_T[rows, pair, h % 2, 1, keys], heads_T[rows, pair, 2, 0],
                                    start=False, stop=True)
                ins.then_inc(scores_done, 1)

            def values(st, ahead, h):
                b, par, _ = st.batch(ahead)
                pair = h // 2
                if h == 0:
                    wait(pe, v_split, 4 * b + 4)
                if h in POOL_HEADS:
                    wait(pe, lo_by_pool, len(POOL_HEADS) * b + POOL_HEADS.index(h) + 1)
                else:
                    wait(pe, lo_by_vector, vector_count(b, h))
                if h % 2 == 0:
                    wait(pe, o_normed, PAIRS * b + pair - 1)
                buf = h % RING
                hi = probs[:, buf].bitcast(BF16)[:, 1::2]
                for t in range(TT):
                    at = (t * 2 + h % 2) * (DH + 1)
                    full = ps_o[:, pair % 2, at:at + DH + 1]
                    for u in range(TT):
                        col = slice(u * seq + t * P, u * seq + (t + 1) * P)
                        pe.matmul(full, hi[:, col], v_hi[:, par, u, h], start=(u == 0), stop=False)
                        pe.matmul(full[:, 0:DH], hi[:, col], v_lo[:, par, u, h], start=False, stop=False)
                        ins = pe.matmul(full, probs_lo[:, buf, col], v_hi[:, par, u, h],
                                        start=False, stop=(u == TT - 1))
                ins.then_inc(attended, 1)

            def result(st, first, count):
                b, par, _ = st.batch(-1)
                n = HC + PAIRS
                for j in range(first, first + count):
                    t, i = j // n, j % n
                    tok, pair = slice(t * P, (t + 1) * P), i - HC
                    o = ps_y[:, tok]
                    if j == 0:
                        wait(pe, gelu_done, 4 * b + 4)
                        wait(pe, y_added, b)
                    if t == 0 and pair >= 0 and pair % 2 == 0:
                        wait(pe, oT_copied, 4 * b + pair // 2 + 1)
                    if pair < 0:
                        ins = pe.matmul(o, hid[:, par, i, tok], w2_eff[:, par, i], start=(i == 0), stop=False)
                    else:
                        ins = pe.matmul(o, oT[:, pair, tok], wo_sb[:, pair], start=False, stop=(i == n - 1))
                if first + count == TT * n:
                    ins.then_inc(y_filled, 1)

            def run(st):
                if st.number == 0:
                    pe.wait_ge(consts_loaded, 16 * 3)
                for s in range(HEADS):
                    if "attn" in st.stages:
                        scores(st, s)
                    for task in aux_tasks(st, s, PER_BATCH):
                        aux(st, *task)
                    if "back" in st.stages and s in Y_PRODUCTS:
                        result(st, sum(Y_PRODUCTS.get(i, 0) for i in range(s)), Y_PRODUCTS[s])
                    late = head_of(st, s, VALUES_LAG)
                    if late:
                        values(st, *late)

            run_all(pe, run)

        @block.scalar
        def _(act):
            def run(st):
                for s in range(HEADS):
                    if "attn" in st.stages:
                        b, par, _ = st.batch(0)
                        buf = s % RING
                        wait(act, scores_done, HEADS * b + s + 1)
                        wait(act, probs_done, HEADS * b + s + 1 - RING)
                        nc.scalar.activation(clamped[:, buf], ps_scores[:, s % SCORE_BANKS], ACT.Tanh).then_inc(clamp_done, 1)
                    late = head_of(st, s, 1)
                    if late:
                        ahead, h = late
                        b, par, _ = st.batch(ahead)
                        buf = h % RING
                        wait(act, clamp_done, HEADS * b + h + 1)
                        wait(act, attended, HEADS * b + h + 1 - RING)
                        nc.scalar.activation(probs[:, buf], clamped[:, buf], ACT.Exp, bias=LIFT,
                                             scale=SOFTCLAMP * DH ** -0.5).then_inc(probs_done, 1)
                    for i, kind, k, ahead in aux_tasks(st, s, ("xhT", "xnT", "qk", "v", "oT", "qkT", "hid")):
                        b, par, _ = st.batch(ahead)
                        bank = ps_aux[:, i % AUX_BANKS, :]
                        act.wait_ge(aux_filled[kind], PER_BATCH[kind] * b + k + 1)
                        if kind == "xhT":
                            nc.scalar.copy(xhT_hi[:, par], bank[:, 0:seq]).then_inc(xT_hi_made, 1)
                        elif kind == "xnT":
                            nc.scalar.copy(xnT[:, par], bank[:, 0:seq]).then_inc(xnT_copied, 1)
                        elif kind == "qk":
                            if k == 0:
                                wait(act, aux_filled["qkT"], PAIRS * (b - 1))
                            t, c = k // 4, k % 4
                            nc.scalar.copy(qk[:, par, t, c * 512:(c + 1) * 512], bank).then_inc(qk_copied, 1)
                        elif kind == "v":
                            if k == 0:
                                wait(act, attended, HEADS * (b - 1))
                            t, c = k // 2, k % 2
                            nc.scalar.copy(v_hi[:, par, t, 8 * c:8 * c + 8, 0:DH],
                                           bank.rearrange("p (h d) -> p h d", d=DH)).then_inc(v_hi_made, 1)
                        elif kind == "oT":
                            nc.scalar.copy(oT[:, 2 * k:2 * k + 2], bank.rearrange("p (j t) -> p j t", j=2))\
                                .then_inc(oT_copied, 1)
                        elif kind == "qkT":
                            nc.scalar.copy(heads_T[:, k, 0].rearrange("p j t -> p (j t)"), bank)\
                                .then_inc(qkT_hi_made, 1)
                        elif kind == "hid":
                            for j in range(2):
                                c = 2 * k + j
                                nc.scalar.activation(hid[:, par, c], bank[:, j * seq:(j + 1) * seq], ACT.Gelu,
                                                     bias=b1_col[:, c:c + 1]).then_inc(gelu_done, 1)

            for c in range(3):
                part = slice(c * HEADS * DH, (c + 1) * HEADS * DH)
                act.wait_ge(w_scaled, c + 1)
                nc.scalar.copy(w_hi[:, part], w_raw[:, part]).then_inc(w_hi_made, 1)
            act.wait_ge(ffn_turned, 1)
            nc.scalar.copy(b1_col[:], ps_o[:, 0, 0:HC]).then_inc(ffn_copied, 1)
            nc.scalar.copy(w1T[:].rearrange("p a b -> p (a b)"), ps_scores[:, 0]).then_inc(ffn_copied, 1)
            nc.scalar.copy(w2T[:].rearrange("p a b -> p (a b)"), ps_scores[:, 1]).then_inc(ffn_copied, 1)
            act.wait_ge(ffn_copied, 3)
            run_all(act, run)

        @block.vector
        def _(dve):
            v = nc.vector
            v.memset(v_hi[:, :, :, :, DH:DH + 1], 1.0)
            def norm_stats(st):
                b, par, half = st.batch(2)
                dve.wait_ge(x_loaded[par], 16 * (half + 1))
                for t in range(TT):
                    v.bn_stats(stats[:, t], x_in[:, par, t]).then_inc(stats_made, 1)

            def norm_var(st):
                b, par, _ = st.batch(2)
                dve.wait_ge(stats_made, 2 * b + 2)
                v.memset(scratch[:], 0.0)
                for t in range(TT):
                    v.bn_aggr(mean_var[:, t], stats[:, t]).then_inc(meanvar_made, 1)

            def norm_eps(st):
                b, par, _ = st.batch(2)
                dve.wait_ge(meanvar_made, 2 * b + 2)
                v.tensor_scalar(var_eps[:, 0], mean_var[:, :, 1], LN_EPS, None, ALU.add).then_inc(vareps_made, 1)
                v.tensor_scalar(var_eps[:, 1], mean_var[:, :, 1], 1.0 + RMS_EPS, RMS_EPS * LN_EPS,
                                ALU.mult, ALU.add).then_inc(vareps_made, 1)

            def norm_apply(st):
                b, par, _ = st.batch(2)
                dve.wait_ge(rstd_made, b + 1)
                wait(dve, aux_filled["xhT"], b)
                wait(dve, aux_filled["xnT"], b - 1)
                wait(dve, rows_loaded, 16 * 6 * (b - 1))
                for j in range(2):
                    for t in range(TT):
                        o = xn[:, par, t] if j == 0 else xh[:, t]
                        ins = v.tensor_scalar(o, x_in[:, par, t], mean_var[:, t, 0:1], rstd[:, j, t:t + 1],
                                              ALU.subtract, ALU.mult)
                ins.then_inc(xn_made, 1)

            def xT_lo(st, bank):
                b, par, _ = st.batch(2)
                dve.wait_ge(xT_hi_made, b + 1)
                v.tensor_tensor(xhT_lo[:, par], bank[:, 0:seq], xhT_hi[:, par].bitcast(F32), ALU.subtract).then_inc(xT_split, 1)

            def sum_squares(st, k):
                b, _, _ = st.batch(1)
                dve.wait_ge(sq_made, 8 * b + k + 1)
                v.tensor_reduce(norm2[:, 8 * k:8 * k + 8], sq[:, k % 2].rearrange("p (h d) -> p h d", d=DH),
                                AX_X, ALU.add).then_inc(norm2_made, 1)

            def rsqrt_safe(st):
                b, _, _ = st.batch(1)
                dve.wait_ge(norm2_made, 8 * b + 8)
                v.tensor_scalar(norm2_safe[:], norm2[:], NORM2_MIN, None, ALU.max).then_inc(seed_made, 1)

            def rsqrt_seed(st):
                b, _, _ = st.batch(1)
                dve.wait_ge(seed_made, 3 * b + 1)
                wait(dve, qk_normed, 4 * b)
                v.tensor_scalar(minus_half_norm2[:], norm2_safe[:], -0.5, None, ALU.mult).then_inc(seed_made, 1)
                v.tensor_scalar(rnorm[:].bitcast(I32), norm2_safe[:].bitcast(I32), -0.5, RSQRT_SEED,
                                ALU.mult, ALU.add).then_inc(seed_made, 1)

            def normalise(st, c):
                b, par, _ = st.batch(1)
                if c == 0:
                    dve.wait_ge(newton_step, 12 * b + 12)
                if c % 2 == 0:
                    dve.wait_ge(q_scaled, 4 * b + c + 2)
                part = qk[:, par].rearrange("p t (j n) -> p (t j) n", j=2)[:, :, c * 4 * DH:(c + 1) * 4 * DH]\
                    .rearrange("p a (h d) -> p a h d", d=DH)
                r = rnorm[:].rearrange("p (a h) -> p a h", h=HEADS)[:, :, 4 * c:4 * c + 4]
                v.tensor_tensor(part, part, r.unsqueeze(3).to_broadcast([P, 2 * TT, 4, DH]), ALU.mult)\
                    .then_inc(qk_normed, 1)

            def lo_part(st, ahead, h):
                b, _, _ = st.batch(ahead)
                buf = h % RING
                dve.wait_ge(probs_done, HEADS * b + h + 1)
                v.tensor_tensor(probs_lo[:, buf], probs[:, buf], probs[:, buf].bitcast(BF16)[:, 1::2], ALU.subtract)\
                    .then_inc(lo_by_vector, 1)

            def divide(st, ahead, pair):
                b, par, _ = st.batch(ahead)
                got = ps_o[:, pair % 2, 0:4 * (DH + 1)].rearrange("p (a d) -> p a d", d=DH + 1)
                dve.wait_ge(attended, HEADS * b + 2 * pair + 2)
                v.reciprocal(rden[:, pair % 2], got[:, :, DH]).then_inc(rden_made, 1)
                dve.wait_ge(rden_made, PAIRS * b + pair + 1)
                if pair == 0:
                    wait(dve, aux_filled["oT"], 4 * (b - 1))
                v.tensor_tensor(o_sb[:, par, :, pair * P:(pair + 1) * P].rearrange("p t (j d) -> p t j d", d=DH),
                                got[:, :, 0:DH].rearrange("p (t j) d -> p t j d", j=2),
                                rden[:, pair % 2].rearrange("p (t j) -> p t j", j=2).unsqueeze(3)
                                .to_broadcast([P, TT, 2, DH]), ALU.mult).then_inc(o_normed, 1)

            def result(st):
                b, par, half = st.batch(-2)
                dve.wait_ge(y_filled, b + 1)
                dve.wait_ge(xb2_made, b + 1)
                wait(dve, y_stored[par], 16 * half)
                v.tensor_tensor(y_sb[:, par].rearrange("p t d -> p (t d)"), ps_y[:, 0:seq],
                                x_b2[:].rearrange("p t d -> p (t d)"), ALU.add).then_inc(y_added, 1)

            def aux(st, i, kind, k, ahead):
                b, par, _ = st.batch(ahead)
                bank = ps_aux[:, i % AUX_BANKS, :]
                if kind == "xhT":
                    xT_lo(st, bank)
                elif kind == "v":
                    dve.wait_ge(v_hi_made, 4 * b + k + 1)
                    t, c = k // 2, k % 2
                    v.tensor_tensor(v_lo[:, par, t, 8 * c:8 * c + 8], bank.rearrange("p (h d) -> p h d", d=DH),
                                    v_hi[:, par, t, 8 * c:8 * c + 8, 0:DH], ALU.subtract).then_inc(v_split, 1)
                elif kind == "qkT":
                    dve.wait_ge(qkT_hi_made, PAIRS * b + k + 1)
                    v.tensor_tensor(heads_T[:, k, 2].rearrange("p j t -> p (j t)"), bank,
                                    heads_T[:, k, 0].rearrange("p j t -> p (j t)"), ALU.subtract)\
                        .then_inc(qkT_split, 1)
                elif kind == "low":
                    dve.wait_ge(aux_filled["low"], 2 * b + k + 1)
                    if k == 1:
                        wait(dve, y_filled, b - 1)
                    o, base = (w1_eff[:], w1T) if k == 0 else (w2_eff[:, par], w2T)
                    v.scalar_tensor_tensor(o, bank.rearrange("p (c n) -> p c n", c=HC), scale_col[:, 0:1], base[:],
                                           ALU.mult, ALU.add)\
                        .then_inc(weff_made, 1)

            def select(st):
                b, _, _ = st.batch(1)
                dve.wait_ge(rows_loaded, 16 * 6 * (b + 1))
                wait(dve, aux_filled["low"], 2 * b)
                v.tensor_copy(sel_rows[:], sel_raw[:]).then_inc(sel_copied, 1)
                dve.wait_ge(sel_copied, 3 * b + 1)
                for at, j in ((BLOCK, 1), (2 * BLOCK, 0)):
                    part = slice(at, at + 2 * RANK)
                    v.tensor_tensor(sel_rows[part, j], sel_raw[part, j], sel_rows[part, j], ALU.subtract)\
                        .then_inc(sel_copied, 1)
                dve.wait_ge(sel_copied, 3 * b + 3)
                even = sel_rows[:, 0]
                v.tensor_tensor(low1[:], even.unsqueeze(1).to_broadcast([ROWS, RANK, P]), mask1[:], ALU.mult)\
                    .then_inc(low_made, 1)
                v.tensor_tensor(low2[:], even.rearrange("p (o t) -> p t o", t=HC).unsqueeze(2)
                                .to_broadcast([ROWS, HC, RANK, P // RANK]), mask2[:], ALU.mult)\
                    .then_inc(low_made, 1)

            def product_of_scales():
                dve.wait_ge(gammas_loaded, 16 * 2)
                v.tensor_scalar(g_raw, g_raw, 1.0, None, ALU.add).then_inc(gammas_made, 1)
                dve.wait_ge(gammas_made, 1)
                v.scalar_tensor_tensor(g_bc[:], g_raw[:, 0], DH / SOFTCLAMP, g_raw[:, 1],
                                       ALU.mult, ALU.mult).then_inc(gammas_made, 1)

            def run(st):
                if st.number == -1:
                    product_of_scales()
                if st.number == 0:
                    dve.wait_ge(consts_loaded, 16 * 3)
                for s in range(HEADS):
                    tasks = list(aux_tasks(st, s, ("xhT", "v", "qkT", "low")))
                    for what, *k in VECTOR_STEPS[s]:
                        if what == "updates":
                            for task in tasks:
                                if task[1] == "low":
                                    aux(st, *task)
                        elif what == "splits":
                            for task in tasks:
                                if task[1] != "low":
                                    aux(st, *task)
                        elif what == "lo":
                            late = head_of(st, s, 1)
                            if late and late[1] not in POOL_HEADS:
                                lo_part(st, *late)
                        elif what == "divide":
                            late = head_of(st, s, VALUES_LAG + 1)
                            if late and late[1] % 2 == 1:
                                divide(st, late[0], late[1] // 2)
                        elif what == "result" and "store" in st.stages:
                            result(st)
                        elif what == "select" and "front" in st.stages:
                            select(st)
                        elif what == "sum" and "front" in st.stages:
                            sum_squares(st, *k)
                        elif what == "seed" and "front" in st.stages:
                            rsqrt_safe(st)
                            rsqrt_seed(st)
                        elif what == "normalise" and "front" in st.stages:
                            normalise(st, *k)
                        elif what == "norm_stats" and "norm" in st.stages:
                            norm_stats(st)
                            norm_var(st)
                            norm_eps(st)
                        elif what == "norm_apply" and "norm" in st.stages:
                            norm_apply(st)

            first = Step(-1, 0, ())
            norm_stats(first)
            norm_var(first)
            norm_eps(first)
            norm_apply(first)
            for c in range(3):
                dve.wait_ge(w_loaded[c], 32 if c == 0 else 16)
                part = w_raw[:, c * HEADS * DH:(c + 1) * HEADS * DH]
                v.tensor_scalar(part, part, nw_col[:, 0:1], None, ALU.mult).then_inc(w_scaled, 1)
            for c in range(3):
                part = slice(c * HEADS * DH, (c + 1) * HEADS * DH)
                dve.wait_ge(w_hi_made, c + 1)
                v.tensor_tensor(w_lo[:, part], w_raw[:, part], w_hi[:, part].bitcast(F32), ALU.subtract)\
                    .then_inc(w_split, 1)
            dve.wait_ge(masks_made, 6)
            dve.wait_ge(ffn_copied, 3)

            run_all(dve, run)

        @block.gpsimd
        def _(pool):
            g = nc.gpsimd
            def norm_rstd(st):
                b, _, _ = st.batch(2)
                pool.wait_ge(vareps_made, 2 * b + 2)
                wait(pool, xn_made, b)
                g.tensor_tensor(rstd[:].rearrange("p a b -> p (a b)"), var_eps[:].rearrange("p a b -> p (a b)"),
                                minus_half[:], ALU.pow).then_inc(rstd_made, 1)

            g.memset(minus_half[:], -0.5).then_inc(minus_half_made, 1)
            pool.wait_ge(minus_half_made, 1)
            norm_rstd(Step(-1, 0, ()))
            g.memset(newton_c[:], 1.5)
            g.memset(sel_raw[:], 0.0).then_inc(rows_cleared, 1)
            g.memset(mask1[:], 0.0)
            g.memset(mask2[:], 0.0)
            g.memset(ident[:], 0.0).then_inc(ident_made, 1)
            pool.wait_ge(ident_made, 1)
            g.affine_select(out=ident[:], in_=ident[:], compare_op=ALU.not_equal, fill=1.0, base=0,
                            pattern=[[-1, P]], channel_multiplier=1).then_inc(ident_made, 1)
            pool.wait_ge(ident_made, 2)
            for i in range(3):
                part = slice(i * BLOCK, i * BLOCK + 2 * RANK)
                if i > 0:
                    pool.wait_ge(masks_made, 2 * i)
                g.affine_select(out=mask1[part], in_=mask1[part], compare_op=ALU.not_equal, fill=1.0, base=0,
                                pattern=[[-1, RANK], [0, P]], channel_multiplier=1).then_inc(masks_made, 1)
                g.affine_select(out=mask2[part], in_=mask2[part], compare_op=ALU.not_equal, fill=1.0, base=-RANK,
                                pattern=[[0, HC], [-1, RANK], [0, P // RANK]], channel_multiplier=1)\
                    .then_inc(masks_made, 1)
            pool.wait_ge(masks_made, 6)

            def square(st, k):
                b, par, _ = st.batch(1)
                t, c = k // 4, k % 4
                part = qk[:, par, t, c * 512:(c + 1) * 512]
                pool.wait_ge(qk_copied, 8 * b + k + 1)
                wait(pool, norm2_made, 8 * b + k - 1)
                g.tensor_tensor(sq[:, k % 2], part, part, ALU.mult).then_inc(sq_made, 1)

            def scale_queries(st, k):
                b, par, _ = st.batch(1)
                t, c = k // 4, k % 4
                part = qk[:, par, t, c * 512:(c + 1) * 512]
                pool.wait_ge(sq_made, 8 * b + k + 1)
                g.tensor_tensor(part, part, g_bc[:, c * 512:(c + 1) * 512], ALU.mult).then_inc(q_scaled, 1)

            def newton(st, turn):
                b, _, _ = st.batch(1)
                if turn == 0:
                    pool.wait_ge(seed_made, 3 * b + 3)
                n = 12 * b + 4 * turn

                def after(k):
                    wait(pool, newton_step, n + k)

                after(0)
                g.tensor_tensor(newton_a[:], rnorm[:], rnorm[:], ALU.mult).then_inc(newton_step, 1)
                after(1)
                g.tensor_tensor(newton_b[:], newton_a[:], minus_half_norm2[:], ALU.mult).then_inc(newton_step, 1)
                after(2)
                g.tensor_tensor(newton_a[:], newton_b[:], newton_c[:], ALU.add).then_inc(newton_step, 1)
                after(3)
                g.tensor_tensor(rnorm[:], rnorm[:], newton_a[:], ALU.mult).then_inc(newton_step, 1)

            def lo_part(st, ahead, h):
                b, _, _ = st.batch(ahead)
                buf = h % RING
                pool.wait_ge(probs_done, HEADS * b + h + 1)
                g.tensor_tensor(probs_lo[:, buf], probs[:, buf], probs[:, buf].bitcast(BF16)[:, 1::2],
                                ALU.subtract).then_inc(lo_by_pool, 1)

            def add_bias(st):
                b, par, half = st.batch(-1)
                pool.wait_ge(res_loaded[par], 16 * (half + 1))
                wait(pool, y_added, b)
                g.tensor_tensor(x_b2[:], x_res[:, par], b2_bc[:].unsqueeze(1).to_broadcast([P, TT, P]),
                                ALU.add).then_inc(xb2_made, 1)

            def run(st):
                if st.number == -1:
                    pool.wait_ge(gammas_made, 2)
                if st.number == 0:
                    pool.wait_ge(consts_loaded, 16 * 3)
                for s in range(HEADS):
                    for what, *k in POOL_STEPS[s]:
                        if what == "lo":
                            late = head_of(st, s, 1)
                            if late and late[1] in POOL_HEADS:
                                lo_part(st, *late)
                        elif what == "square" and "front" in st.stages:
                            square(st, *k)
                        elif what == "scale" and "front" in st.stages:
                            scale_queries(st, *k)
                        elif what == "newton" and "front" in st.stages:
                            newton(st, *k)
                        elif what == "bias" and "back" in st.stages:
                            add_bias(st)
                        elif what == "rstd" and "norm" in st.stages:
                            norm_rstd(st)

            run_all(pool, run)


_INS = ["L0_attn_tokens", "L0_attn_norm_w", "L0_attn_Wq", "L0_attn_Wkv", "L0_attn_Wo", "L0_attn_q_gamma",
        "L0_attn_k_gamma", "L0_ffn_W1", "L0_ffn_b1", "L0_ffn_W2", "L0_ffn_b2", "L0_ffn_scale"]


def kernel(**inputs):
    import numpy as _np
    import concourse.bacc as _bacc
    from concourse import mybir as _mybir
    from concourse.bass_utils import run_bass_kernel_spmd as _run

    nc = _bacc.Bacc("TRN2", target_bir_lowering=False, num_devices=1)
    arrays, args = {}, []
    for name in _INS:
        a = _np.ascontiguousarray(inputs[name])
        if a.ndim == 0:
            a = a.reshape(1)
        arrays[f"in_{name}_dram"] = a
        args.append(nc.dram_tensor(f"in_{name}_dram", a.shape, _mybir.dt.from_np(a.dtype), kind="ExternalInput").ap())
    shape = tuple(inputs["L0_attn_tokens"].shape)
    out = nc.dram_tensor("out_0_dram", shape, _mybir.dt.float32, kind="ExternalOutput").ap()
    block_kernel(nc, *args, out)
    r = _run(nc, [arrays], core_ids=[0])
    return r.results[0]["out_0_dram"]
```
